# Optimizing a Trainium2 kernel written in Bass

```python
import numpy as np
import jax
import jax.numpy as jnp

def _softmax(x, axis=-1):
    return jax.nn.softmax(x, axis=axis)

def _gelu(x):
    return jax.nn.gelu(x, approximate=True)

def _silu(x):
    return jax.nn.silu(x)

def _sigmoid(x):
    return jax.nn.sigmoid(x)

def _layernorm(x, axis=-1, eps=1e-05):
    m = jnp.mean(x, axis=axis, keepdims=True)
    v = jnp.var(x, axis=axis, keepdims=True)
    return (x - m) / jnp.sqrt(v + eps)

def _scatter_add(tgt, idx, src, axis=0):
    return tgt.at[idx].add(src)

def _segment_sum(src, seg, n):
    return jax.ops.segment_sum(src, seg, n)
kernel_name = 'mk_vit_tower_d1_tok_img1024_r4_d2c3ae'

def setup_inputs(seed: int=0):
    np.random.seed(seed)
    _w = jnp.asarray

    def _rec_inputs():
        import jax
        import jax.numpy as jnp
        _rk = jax.random.key(seed)
        x = -0.000222058 + 0.999998 * jax.random.normal(jax.random.fold_in(_rk, 1), (16, 3, 96, 96), jnp.float32)
        return x
    x = _rec_inputs()

    def _L0_tok_setup():
        import jax, jax.numpy as jnp
        import numpy as np
        P = 16
        C = 3
        D = 256

        def _patchify(x, p):
            B, Cc, H, W = x.shape
            gh, gw = (H // p, W // p)
            x = x.reshape(B, Cc, gh, p, gw, p)
            x = x.transpose(0, 2, 4, 1, 3, 5)
            return x.reshape(B, gh * gw, Cc * p * p)
        key = jax.random.key(seed)
        k1, k2, k3, k4, k5 = jax.random.split(key, 5)
        patch_dim = C * P * P
        s1 = 1.0 / np.sqrt(patch_dim)
        s2 = 1.0 / np.sqrt(D)
        return {'x': jax.random.normal(k1, (32, C, 128, 128), dtype=jnp.float32), 'W1': jax.random.uniform(k2, (patch_dim, D), jnp.float32, -s1, s1), 'b1': jax.random.uniform(k3, (D,), jnp.float32, -s1, s1), 'W2': jax.random.uniform(k4, (D, D), jnp.float32, -s2, s2), 'b2': jax.random.uniform(k5, (D,), jnp.float32, -s2, s2)}
    _L0_tok_all = _L0_tok_setup()
    _L0_tok_in = {k: v for k, v in _L0_tok_all.items() if k in ('W1', 'b1', 'W2', 'b2')}
    del _L0_tok_all

    def _L0_attn_setup():
        import jax, jax.numpy as jnp
        import numpy as np
        import math
        B, S, D = (4, 512, 256)
        H, DEG, DH, BUS, SLOTS = (8, 4, 32, 128, 64)
        EPS = 1.1920929e-07

        def _rms(x, w):
            return x * jax.lax.rsqrt(jnp.mean(x * x, axis=-1, keepdims=True) + EPS) * w
        key = jax.random.key(seed)
        ks = jax.random.split(key, 20)
        g = lambda k, shape, s=0.02: jax.random.normal(k, shape, jnp.float32) * s
        return {'x': jax.random.normal(ks[0], (B, S, D), jnp.float32), 'w_norm_in': jnp.ones((D,), jnp.float32), 'w_norm_out': jnp.ones((D,), jnp.float32), 'router_w1': g(ks[1], (D, D // 2)), 'router_w2': g(ks[2], (D // 2, 3)), 'router_b2': jnp.full((3,), 0.5, jnp.float32), 'ttt_w1': g(ks[3], (D, D // 4)), 'ttt_b1': jnp.zeros((D // 4,), jnp.float32), 'ttt_w2': g(ks[4], (D // 4, H * DEG)), 'ttt_b2': jnp.zeros((H * DEG,), jnp.float32), 'lambdas': jnp.array([0.9995, 0.9995, 0.997, 0.997, 0.995, 0.995, 0.97, 0.95], jnp.float32), 'slr_wq1': g(ks[5], (D, DH)), 'slr_wq2': g(ks[6], (D, DH)), 'slr_wk1': g(ks[7], (D, DH)), 'slr_wk2': g(ks[8], (D, DH)), 'slr_wv': g(ks[9], (D, DH)), 'slr_wo': g(ks[10], (DH, D)), 'slr_lam': jnp.array(0.5, jnp.float32), 'landmarks': g(ks[11], (SLOTS, D), 0.5), 'mix_w': g(ks[12], (2 * D, D)), 'bus_compress': g(ks[13], (D, BUS)), 'bus_expand': g(ks[14], (BUS, D)), 'bus_publish': g(ks[15], (BUS, BUS))}
    _L0_attn_all = _L0_attn_setup()
    _L0_attn_in = {k: v for k, v in _L0_attn_all.items() if k in ('w_norm_in', 'w_norm_out', 'router_w1', 'router_w2', 'router_b2', 'ttt_w1', 'ttt_b1', 'ttt_w2', 'ttt_b2', 'lambdas', 'slr_wq1', 'slr_wq2', 'slr_wk1', 'slr_wk2', 'slr_wv', 'slr_wo', 'slr_lam', 'landmarks', 'mix_w', 'bus_compress', 'bus_expand', 'bus_publish')}
    del _L0_attn_all

    def _L0_ffn_setup():
        import jax, jax.numpy as jnp
        import numpy as np
        import math
        BETA = 0.9
        THRESHOLD = 1.0
        NUM_STEPS = 5
        ALPHA = 2.0

        @jax.custom_vjp
        def spike_fn(u):
            return (u > 0).astype(u.dtype)

        def _spike_fwd(u):
            return (spike_fn(u), u)

        def _spike_bwd(u, g):
            s = jnp.pi / 2.0 * ALPHA * u
            return (g * (ALPHA / 2.0) / (1.0 + s * s),)
        spike_fn.defvjp(_spike_fwd, _spike_bwd)
        key = jax.random.key(seed)
        k1, k2, k3 = jax.random.split(key, 3)
        n_embd = 256
        x = jax.random.normal(k1, (4, 512, n_embd), dtype=jnp.float32)
        W_fc = jax.random.normal(k2, (4 * n_embd, n_embd), dtype=jnp.float32) / math.sqrt(n_embd)
        W_proj = jax.random.normal(k3, (n_embd, 4 * n_embd), dtype=jnp.float32) / math.sqrt(4 * n_embd)
        return {'x': x, 'W_fc': W_fc, 'W_proj': W_proj}
    _L0_ffn_all = _L0_ffn_setup()
    _L0_ffn_in = {k: v for k, v in _L0_ffn_all.items() if k in ('W_fc', 'W_proj')}
    del _L0_ffn_all
    return {'x': x, 'L0_tok_W1': _L0_tok_in['W1'], 'L0_tok_b1': _L0_tok_in['b1'], 'L0_tok_W2': _L0_tok_in['W2'], 'L0_tok_b2': _L0_tok_in['b2'], 'L0_attn_w_norm_in': _L0_attn_in['w_norm_in'], 'L0_attn_w_norm_out': _L0_attn_in['w_norm_out'], 'L0_attn_router_w1': _L0_attn_in['router_w1'], 'L0_attn_router_w2': _L0_attn_in['router_w2'], 'L0_attn_router_b2': _L0_attn_in['router_b2'], 'L0_attn_ttt_w1': _L0_attn_in['ttt_w1'], 'L0_attn_ttt_b1': _L0_attn_in['ttt_b1'], 'L0_attn_ttt_w2': _L0_attn_in['ttt_w2'], 'L0_attn_ttt_b2': _L0_attn_in['ttt_b2'], 'L0_attn_lambdas': _L0_attn_in['lambdas'], 'L0_attn_slr_wq1': _L0_attn_in['slr_wq1'], 'L0_attn_slr_wq2': _L0_attn_in['slr_wq2'], 'L0_attn_slr_wk1': _L0_attn_in['slr_wk1'], 'L0_attn_slr_wk2': _L0_attn_in['slr_wk2'], 'L0_attn_slr_wv': _L0_attn_in['slr_wv'], 'L0_attn_slr_wo': _L0_attn_in['slr_wo'], 'L0_attn_slr_lam': _L0_attn_in['slr_lam'], 'L0_attn_landmarks': _L0_attn_in['landmarks'], 'L0_attn_mix_w': _L0_attn_in['mix_w'], 'L0_attn_bus_compress': _L0_attn_in['bus_compress'], 'L0_attn_bus_expand': _L0_attn_in['bus_expand'], 'L0_attn_bus_publish': _L0_attn_in['bus_publish'], 'L0_ffn_W_fc': _L0_ffn_in['W_fc'], 'L0_ffn_W_proj': _L0_ffn_in['W_proj']}

def reference(x, L0_tok_W1, L0_tok_b1, L0_tok_W2, L0_tok_b2, L0_attn_w_norm_in, L0_attn_w_norm_out, L0_attn_router_w1, L0_attn_router_w2, L0_attn_router_b2, L0_attn_ttt_w1, L0_attn_ttt_b1, L0_attn_ttt_w2, L0_attn_ttt_b2, L0_attn_lambdas, L0_attn_slr_wq1, L0_attn_slr_wq2, L0_attn_slr_wk1, L0_attn_slr_wk2, L0_attn_slr_wv, L0_attn_slr_wo, L0_attn_slr_lam, L0_attn_landmarks, L0_attn_mix_w, L0_attn_bus_compress, L0_attn_bus_expand, L0_attn_bus_publish, L0_ffn_W_fc, L0_ffn_W_proj):
    import jax
    import jax.numpy as jnp

    def _L0_tok_ref(x, W1, b1, W2, b2):
        import jax, jax.numpy as jnp
        import numpy as np
        P = 16
        C = 3
        D = 256

        def _patchify(x, p):
            B, Cc, H, W = x.shape
            gh, gw = (H // p, W // p)
            x = x.reshape(B, Cc, gh, p, gw, p)
            x = x.transpose(0, 2, 4, 1, 3, 5)
            return x.reshape(B, gh * gw, Cc * p * p)
        patches = _patchify(x, P)
        h = jax.nn.silu(jnp.einsum('blk,kd->bld', patches, W1) + b1)
        return jnp.einsum('bld,de->ble', h, W2) + b2

    def _L0_attn_ref(x, w_norm_in, w_norm_out, router_w1, router_w2, router_b2, ttt_w1, ttt_b1, ttt_w2, ttt_b2, lambdas, slr_wq1, slr_wq2, slr_wk1, slr_wk2, slr_wv, slr_wo, slr_lam, landmarks, mix_w, bus_compress, bus_expand, bus_publish):
        import jax, jax.numpy as jnp
        import numpy as np
        import math
        B, S, D = (4, 512, 256)
        H, DEG, DH, BUS, SLOTS = (8, 4, 32, 128, 64)
        EPS = 1.1920929e-07

        def _rms(x, w):
            return x * jax.lax.rsqrt(jnp.mean(x * x, axis=-1, keepdims=True) + EPS) * w
        b, s, d = x.shape
        hd = d // H
        residual = x
        xn = _rms(x, w_norm_in)
        route_in = xn.mean(axis=1)
        logits = jax.nn.silu(route_in @ router_w1) @ router_w2 + router_b2
        probs = jax.nn.softmax(logits, axis=-1)
        p_medium, p_full = (probs[:, 1], probs[:, 2])
        ttt = (jax.nn.silu(route_in @ ttt_w1 + ttt_b1) @ ttt_w2 + ttt_b2).reshape(b, H, DEG)
        ttt_scale = 0.1 * jnp.tanh(ttt)
        xh = xn.reshape(b, s, H, hd).transpose(1, 0, 2, 3)
        lam = lambdas[None, :, None]

        def ema_step(state, xt):
            state = lam * state + (1.0 - lam) * xt
            return (state, state)
        _, ys = jax.lax.scan(ema_step, jnp.zeros((b, H, hd), x.dtype), xh)
        ssm_out = ys.transpose(1, 0, 2, 3).reshape(b, s, d)
        q1, q2 = (xn @ slr_wq1, xn @ slr_wq2)
        k1, k2 = (xn @ slr_wk1, xn @ slr_wk2)
        v = xn @ slr_wv
        sc = 1.0 / math.sqrt(DH)
        a1 = jax.nn.softmax(jnp.einsum('bqd,bkd->bqk', q1, k1) * sc, axis=-1)
        a2 = jax.nn.softmax(jnp.einsum('bqd,bkd->bqk', q2, k2) * sc, axis=-1)
        ctx = jnp.einsum('bqk,bkd->bqd', a1 - slr_lam * a2, v)
        slr_out = ctx @ slr_wo
        mixed = ssm_out + (p_medium + p_full)[:, None, None] * slr_out
        qy = xn[:, -1:, :]
        kk = jnp.broadcast_to(landmarks[None], (b, SLOTS, d))
        attn = jax.nn.softmax(jnp.einsum('bqd,bkd->bqk', qy, kk) / math.sqrt(d), axis=-1)
        arc_ctx = jnp.einsum('bqk,bkd->bqd', attn, kk)
        mixed = mixed.at[:, -1:, :].add(p_full[:, None, None] * arc_ctx)
        out = jnp.concatenate([mixed, xn], axis=-1) @ mix_w
        out = residual + _rms(out, w_norm_out)
        summary = out.mean(axis=1, keepdims=True) @ bus_compress
        published = summary @ bus_publish
        aw = jax.nn.softmax(jnp.einsum('bqd,bkd->bqk', summary, published) / math.sqrt(BUS), axis=-1)
        context = jnp.einsum('bqk,bkd->bqd', aw, published)
        out = out + 0.1 * (context @ bus_expand)
        return out

    def _L0_ffn_ref(x, W_fc, W_proj):
        import jax, jax.numpy as jnp
        import numpy as np
        import math
        BETA = 0.9
        THRESHOLD = 1.0
        NUM_STEPS = 5
        ALPHA = 2.0

        @jax.custom_vjp
        def spike_fn(u):
            return (u > 0).astype(u.dtype)

        def _spike_fwd(u):
            return (spike_fn(u), u)

        def _spike_bwd(u, g):
            s = jnp.pi / 2.0 * ALPHA * u
            return (g * (ALPHA / 2.0) / (1.0 + s * s),)
        spike_fn.defvjp(_spike_fwd, _spike_bwd)
        h = jnp.square(jax.nn.relu(jnp.einsum('bsd,fd->bsf', x, W_fc)))
        y = jnp.einsum('bsf,df->bsd', h, W_proj)

        def step(mem, _):
            reset = jax.lax.stop_gradient(spike_fn(mem - THRESHOLD))
            mem_new = BETA * mem + y - reset * THRESHOLD
            spk = spike_fn(mem_new - THRESHOLD)
            return (mem_new, spk)
        mem0 = jnp.zeros_like(y)
        _, spks = jax.lax.scan(step, mem0, None, length=NUM_STEPS)
        return jnp.sum(spks, axis=0) / NUM_STEPS
    h = _L0_tok_ref(x, L0_tok_W1, L0_tok_b1, L0_tok_W2, L0_tok_b2)
    h = h + _L0_attn_ref(_layernorm(h, axis=-1), L0_attn_w_norm_in, L0_attn_w_norm_out, L0_attn_router_w1, L0_attn_router_w2, L0_attn_router_b2, L0_attn_ttt_w1, L0_attn_ttt_b1, L0_attn_ttt_w2, L0_attn_ttt_b2, L0_attn_lambdas, L0_attn_slr_wq1, L0_attn_slr_wq2, L0_attn_slr_wk1, L0_attn_slr_wk2, L0_attn_slr_wv, L0_attn_slr_wo, L0_attn_slr_lam, L0_attn_landmarks, L0_attn_mix_w, L0_attn_bus_compress, L0_attn_bus_expand, L0_attn_bus_publish)
    h = h + _L0_ffn_ref(_layernorm(h, axis=-1), L0_ffn_W_fc, L0_ffn_W_proj)
    return h

_drawn_inputs = setup_inputs


def setup_inputs(seed=0):
    import zlib

    import numpy as np

    out = dict(_drawn_inputs(seed))
    spreads = {'L0_attn_w_norm_in': (1.0, 0.2),
     'L0_attn_w_norm_out': (1.0, 0.2),
     'L0_attn_router_b2': (0.5, 0.6),
     'L0_attn_ttt_b1': (0.0, 0.1),
     'L0_attn_ttt_b2': (0.0, 0.1)}
    factors = {'L0_attn_router_w1': 8.0,
     'L0_attn_router_w2': 8.0,
     'L0_attn_slr_wq1': 8.0,
     'L0_attn_slr_wq2': 8.0,
     'L0_attn_slr_wk1': 8.0,
     'L0_attn_slr_wk2': 8.0,
     'L0_attn_slr_wv': 8.0,
     'L0_attn_slr_wo': 8.0,
     'L0_attn_landmarks': 8.0,
     'L0_attn_bus_compress': 8.0,
     'L0_attn_bus_expand': 8.0,
     'L0_attn_bus_publish': 8.0}
    for name, (base, spread) in spreads.items():
        noise = np.random.default_rng([zlib.crc32(name.encode()), seed]).standard_normal(out[name].shape)
        drawn = base * np.exp(spread * noise) if base else spread * noise
        out[name] = jnp.asarray(drawn.astype(out[name].dtype))
    for name, factor in factors.items():
        out[name] = (out[name] * factor).astype(out[name].dtype)
    return out
```

```python
from contextlib import ExitStack

import numpy as np

import concourse.bass as bass
from concourse import mybir

ALU = mybir.AluOpType
ACT = mybir.ActivationFunctionType
F32 = mybir.dt.float32
AX = mybir.AxisListType

P = 128
D = 256
DF = D // P
B = 16
GRID = 6
S = GRID * GRID
T = B * S
PATCH = 16
KP = 3 * PATCH * PATCH // P
NC = 2
CH = T // NC
NT = -(-T // P)
DH = 32
SLOTS = 64
BUS = 128
F = 1024
MF = F // P
PAIR = 2 * S
NPAIR = B // 2
HALF = 64
HEADS = 8
EPS_LN = 1e-5
EPS_RMS = 1.1920929e-07
BETA, THRESHOLD, NUM_STEPS = 0.9, 1.0, 5

W2_AT, B2_AT, VEC_AT = 0, DF * D, DF * D + D
VEC = 3 * DF + 3 + 1
PACK_A = VEC_AT + VEC
QK_AT = 0
V_AT = QK_AT + DF * P
R1_AT = V_AT + DF * DH
LW_AT = R1_AT + DF * P
R2_AT = LW_AT + DF * (SLOTS + DH)
WO_AT = R2_AT + 3
PACK_B = WO_AT + D
BUS_AT = 2 * DF * D
PACK_C = BUS_AT + D + BUS + D
PACK_F = DF * F
PACK_P = MF * D


def tokens(t):
    return t * P, min(P, T - t * P)


def tiles_before(token):
    return -(-token // P)


def spike_thresholds():
    f = np.float32

    def count(y):
        mem, spikes = f(0), 0
        for _ in range(NUM_STEPS):
            reset = f(mem - f(THRESHOLD) > 0)
            mem = f(f(f(BETA) * mem) + y) - reset * f(THRESHOLD)
            spikes += int(mem - f(THRESHOLD) > 0)
        return spikes

    steps = []
    for n in range(1, NUM_STEPS + 1):
        low, high = f(0), f(2 * THRESHOLD)
        while np.nextafter(low, high) < high:
            mid = f((low + high) / 2)
            if count(mid) >= n:
                high = mid
            else:
                low = mid
        steps.append(float(low))
    return steps


def build(nc, pw_d, a_d, b_d, c_d, f_d, p_d, out_d):
    thresholds = spike_thresholds()
    ctx = ExitStack()
    with ctx:
        def sb(name, shape):
            return ctx.enter_context(nc.sbuf_tensor(name, shape, F32))

        def sem(name):
            return ctx.enter_context(nc.semaphore(name))

        pw = sb("patches_and_w1", [P, KP, T + D])
        wa = sb("pack_a", [P, PACK_A])
        wb = sb("pack_b", [P, PACK_B])
        wc = sb("pack_c", [P, PACK_C])
        wf = sb("w_fc", [P, DF, F])
        wp = sb("w_proj", [P, MF, D])
        w2 = wa[:, W2_AT:B2_AT].rearrange("p (k n) -> p k n", k=DF)
        b2 = wa[:, B2_AT:VEC_AT]
        vec = wa[:, VEC_AT:PACK_A]
        b1, w_in, lam = vec[:, 0:2], vec[:, 2:4], vec[:, 4:6]
        rb2, slr_lam = vec[:, 6:9], vec[:, 9:10]
        wqk = wb[:, QK_AT:V_AT].rearrange("p (k n) -> p k n", k=DF)
        wv = wb[:, V_AT:R1_AT].rearrange("p (k n) -> p k n", k=DF)
        rw1 = wb[:, R1_AT:LW_AT].rearrange("p (k n) -> p k n", k=DF)
        lmwo = wb[:, LW_AT:R2_AT].rearrange("p (k n) -> p k n", k=DF)
        rw2 = wb[:, R2_AT:WO_AT]
        w_out = wb[:, WO_AT:PACK_B]
        mix = wc[:, 0:BUS_AT].rearrange("p (k n) -> p k n", k=2 * DF)
        compress_t = wc[:, BUS_AT:BUS_AT + D]
        publish_t = wc[:, BUS_AT + D:BUS_AT + D + BUS]
        expand = wc[:, BUS_AT + D + BUS:PACK_C]

        ident = sb("ident", [P, P])
        image_mean = sb("image_mean", [P, NT, B])
        minus_half = sb("minus_half", [P, 2])
        lam_scan = sb("lam_scan", [P, DF, T])
        one_minus_lam = sb("one_minus_lam", [P, DF])
        mix_ssm = sb("mix_ssm", [P, DF, D])
        rw2_b = sb("rw2_b", [P, 3, P])
        neg_lam = sb("neg_lam", [P, 1])

        hidden = sb("hidden", [P, DF, T])
        h0 = sb("h0", [P, NT, D])
        stats = sb("stats", [P, NT, 6])
        mv = sb("mv", [P, NT, 2])
        ve = sb("ve", [P, NT, 2])
        rs = sb("rs", [P, NT, 2])
        xhat = sb("xhat", [P, NT, D])
        xT = sb("xT", [P, DF, T])
        a = sb("a", [P, NT, D])
        lmwo_mix = sb("lmwo_mix", [SLOTS + DH, D])
        pub_exp = sb("pub_exp", [BUS, D])
        bus_w = sb("bus_w", [P, DF, D])
        qs = sb("qs", [2 * DH, T + HALF - S])
        ks = sb("ks", [2 * DH, T])
        vs = sb("vs", [PAIR, NPAIR, DH])
        route = sb("route", [P, DF, B])
        rhid = sb("rhid", [P, B])
        lg = sb("lg", [P, B, 3])
        lgm = sb("lgm", [P, B])
        lge = sb("lge", [P, B, 3])
        lgs = sb("lgs", [P, B])
        lgr = sb("lgr", [P, B])
        gate = sb("gate", [P, B])
        gsum = sb("gsum", [P, B])
        p_full = sb("p_full", [P, B])
        smax = sb("smax", [P, 2, NPAIR])
        sh = sb("sh", [P, 2, NPAIR, S])
        se = sb("se", [P, 2, NPAIR, S])
        ssum = sb("ssum", [P, 2, NPAIR])
        srec = sb("srec", [P, 2, NPAIR])
        sfac = sb("sfac", [P, NPAIR])
        sp = sb("sp", [P, 2, NPAIR, S])
        probs = sb("probs", [P, NPAIR, PAIR])
        probs_t = sb("probs_t", [PAIR, NPAIR, PAIR])
        arc_m = sb("arc_m", [B, 1])
        arc_b = sb("arc_b", [B, 1])
        arc_e = sb("arc_e", [B, SLOTS])
        arc_s = sb("arc_s", [B, 1])
        arc_r = sb("arc_r", [B, 1])
        arc_p = sb("arc_p", [B, SLOTS])
        comb = sb("comb", [SLOTS + DH, T])
        ssm = sb("ssm", [P, DF, T])
        sqj = sb("sqj", [P, D])
        ssq = sb("ssq", [P, NT])
        rve = sb("rve", [P, NT])
        rr = sb("rr", [P, NT])
        rms = sb("rms", [P, NT, D])
        out2 = sb("out2", [P, NT, D])
        h1p = sb("h1p", [P, NT, D])
        mean_b = sb("mean_b", [P, DF, B, S])
        h1 = sb("h1", [P, NT, D])
        stats2 = sb("stats2", [P, NT, 6])
        mv2 = sb("mv2", [P, NT, 2])
        ve2 = sb("ve2", [P, NT])
        rs2 = sb("rs2", [P, NT])
        yhat = sb("yhat", [P, NT, D])
        fT = sb("fT", [P, DF, T])
        relu = sb("relu", [P, 2, CH])
        hid2 = sb("hid2", [P, MF, T])
        count = sb("count", [P, NT, NUM_STEPS, D])
        result = sb("result", [P, NT, D])

        bank = [ctx.enter_context(nc.psum_tensor(f"bank{i}", [P, 512], F32)) for i in range(8)]

        def ps_z(m, c):
            return bank[2 * m + c][:, 0:CH]

        def ps_h(t):
            return bank[4 + t % 2][:, 0:D]

        def ps_xt(t, f):
            return bank[(6 + t % 2, 3 * (t % 2))[f]][:, 0:P]

        ps_lw = bank[1][0:SLOTS + DH, 0:D]
        ps_pe = bank[2][:, 0:D]
        ps_bus = bank[1][:, :].rearrange("p (f n) -> p f n", f=DF)
        ps_qk = [bank[4][:, 0:CH], bank[5][:, 0:CH]]
        ps_v = bank[2][0:PAIR, 0:NPAIR * DH]
        ps_r = bank[6][:, 0:B]
        ps_lg = bank[6][:, 64:64 + 3 * B].rearrange("p (j b) -> p j b", j=3)
        ps_arc = bank[7][0:B, 0:SLOTS]
        ps_arct = bank[7][0:SLOTS, 64:64 + B]
        ps_s = [bank[i][:, 0:NPAIR * S].rearrange("p (j k) -> p j k", j=NPAIR) for i in range(2)]
        ps_pt = [bank[2 + i][0:PAIR, :].rearrange("p (j q) -> p j q", j=NPAIR // 2) for i in range(2)]
        ps_c = [bank[4 + i][SLOTS:SLOTS + DH, 0:CH] for i in range(2)]
        O_BANKS = [0, 1, 2, 3, 6]
        X_BANKS = [7, 0, 1, 2, 3]
        YT_BANKS = [4, 5, 6, 4, 5]
        FC_BANKS = [7, 0, 1, 2]
        Y_BANKS = [3, 4, 5, 6, 7]
        ps_m = [bank[4 + f][:, 0:B] for f in range(DF)]

        def ps_o(t):
            return bank[O_BANKS[t]][:, 0:D]

        def ps_x(t):
            return bank[X_BANKS[t]][:, 0:D]

        def ps_yt(t):
            return bank[YT_BANKS[t]][:, 0:D].rearrange("p (f n) -> p f n", f=DF)

        def ps_f(i):
            return bank[FC_BANKS[i % len(FC_BANKS)]][:, 0:CH]

        def ps_y(t):
            return bank[Y_BANKS[t]][:, 0:D]

        names = """a_in b_in c_in f_in p_in const_zero const_ready lam_prep mixs_ready rw2b_ready
        z_ready hidden_ready h_ready h0_ready stats_ready mv_ready ve_ready rs_ready xhat_ready
        xt_ready xt_act xt_dve a_ready lw_ready pe_ready bus_ready lw_taken pe_taken bus_taken
        qk_ready q_taken k_taken v_ready v_taken route_ready r_ready rhid_ready lg_ready lg_chain
        lg_shift lg_exp gate_ready pfull_ready s_ready smax_ready sh_ready se_ready ssum_ready
        srec_ready sfac_ready neg_ready sp_ready probs_ready pt_ready pt_act pt_dve c_ready c_taken
        arc_ready arcm_ready arcb_ready arce_ready arcr_ready arcp_ready arct_ready arc_taken
        ssm_ready o_ready ssq_ready rve_ready rr_ready rms_ready out2_ready h1p_ready m_ready
        meanb_ready x_ready h1_ready stats2_ready mv2_ready ve2_ready rs2_ready yhat_ready yt_ready
        ft_act fc_ready relu_ready hid2_ready y_ready count_ready result_ready out_sem
        pad_ready""".split()
        s = {n: sem(n) for n in names}
        pw_in = [sem(f"pw_in{k}") for k in range(KP)]
        const_ready, lam_prep = s["const_ready"], s["lam_prep"]

        block = ctx.enter_context(nc.Block())

        @block.sync
        def _(sp_):
            for k in range(KP):
                sp_.dma_start(pw[:, k, :], pw_d[:, k, :]).then_inc(pw_in[k], 16)
                if k == 2:
                    sp_.dma_start(wa[:, :], a_d).then_inc(s["a_in"], 16)
            sp_.dma_start(wb[:, :], b_d).then_inc(s["b_in"], 16)
            sp_.dma_start(wc[:, :], c_d).then_inc(s["c_in"], 16)
            sp_.dma_start(wf[:, :, :], f_d).then_inc(s["f_in"], 16)
            sp_.dma_start(wp[:, :, :], p_d).then_inc(s["p_in"], 16)
            for t in range(NT):
                t0, n = tokens(t)
                sp_.wait_ge(s["result_ready"], t + 1)
                sp_.dma_start(out_d[t0:t0 + n, :], result[0:n, t, :]).then_inc(s["out_sem"], 16)
            sp_.wait_ge(s["out_sem"], 16 * NT)

        def sum_h1p(t, pool, g):
            _, n = tokens(t)
            pool.wait_ge(s["out2_ready"], t + 1)
            g.tensor_tensor(h1p[0:n, t, :], out2[0:n, t, :], h0[0:n, t, :], ALU.add).then_inc(s["h1p_ready"], 1)

        @block.gpsimd
        def _(pool):
            g = nc.gpsimd
            g.memset(ident[:, :], 0.0).then_inc(s["const_zero"], 1)
            g.memset(image_mean[:, :, :], 1.0 / S).then_inc(s["const_zero"], 1)
            g.memset(minus_half[:, :], -0.5).then_inc(const_ready, 1)
            pool.wait_ge(s["const_zero"], 2)
            g.affine_select(out=ident[:, :], in_=ident[:, :], compare_op=ALU.not_equal, fill=1.0,
                            base=0, pattern=[[-1, P]], channel_multiplier=1).then_inc(const_ready, 1)
            g.affine_select(out=image_mean[:, :, :], in_=image_mean[:, :, :], compare_op=ALU.is_ge,
                            fill=0.0, base=0, pattern=[[P, NT], [-S, B]],
                            channel_multiplier=1).then_inc(s["const_zero"], 1)
            pool.wait_ge(s["const_zero"], 3)
            g.affine_select(out=image_mean[:, :, :], in_=image_mean[:, :, :], compare_op=ALU.is_ge,
                            fill=0.0, base=S - 1, pattern=[[-P, NT], [S, B]],
                            channel_multiplier=-1).then_inc(const_ready, 1)
            g.memset(probs[:, :, :], 0.0).then_inc(s["pad_ready"], 1)
            g.memset(comb[0:SLOTS, :], 0.0).then_inc(s["pad_ready"], 1)
            g.memset(qs[:, T:T + HALF - S], 0.0).then_inc(s["pad_ready"], 1)

            pool.wait_ge(s["a_in"], 16)
            for f in range(DF):
                g.tensor_copy(lam_scan[:, f, :], lam[:, f:f + 1].to_broadcast([P, T])).then_inc(lam_prep, 1)
            pool.wait_ge(lam_prep, DF)
            for f in range(DF):
                g.memset(lam_scan[:, f, :].rearrange("p (b s) -> p b s", s=S)[:, :, 0:1], 0.0).then_inc(lam_prep, 1)
            g.tensor_scalar(one_minus_lam[:, :], lam, -1.0, 1.0, ALU.mult, ALU.add).then_inc(lam_prep, 1)

            def power(out, in_, exps, after, n, ready):
                pool.wait_ge(after, n)
                g.tensor_tensor(out, in_, exps, ALU.pow).then_inc(ready, 1)

            for t in range(NT):
                _, n = tokens(t)
                power(rs[0:n, t, :], ve[0:n, t, :], minus_half[0:n, :], s["ve_ready"], t + 1, s["rs_ready"])
            pool.wait_ge(s["b_in"], 16)
            for j in range(3):
                g.tensor_copy(rw2_b[:, j, :], rw2[:, j:j + 1].to_broadcast([P, P])).then_inc(s["rw2b_ready"], 1)
            pool.wait_ge(s["c_in"], 16)
            for f in range(DF):
                g.tensor_scalar(mix_ssm[:, f, :], mix[:, f, :], one_minus_lam[:, f:f + 1], None,
                                ALU.mult).then_inc(s["mixs_ready"], 1)
            for t in range(NT):
                _, n = tokens(t)
                pool.wait_ge(s["rs_ready"], t + 1)
                g.tensor_scalar(a[0:n, t, :], h0[0:n, t, :], mv[0:n, t, 0:1], rs[0:n, t, 0:1],
                                ALU.subtract, ALU.mult).then_inc(s["a_ready"], 1)
            for t in range(NT):
                _, n = tokens(t)
                power(rr[0:n, t:t + 1], rve[0:n, t:t + 1], minus_half[0:n, 0:1], s["rve_ready"], t + 1, s["rr_ready"])
                if t >= 1:
                    sum_h1p(t - 1, pool, g)
            sum_h1p(NT - 1, pool, g)
            for t in range(NT):
                _, n = tokens(t)
                power(rs2[0:n, t:t + 1], ve2[0:n, t:t + 1], minus_half[0:n, 0:1], s["ve2_ready"], t + 1, s["rs2_ready"])

        @block.scalar
        def _(act):
            e = nc.scalar
            act.wait_ge(s["a_in"], 16)
            for c in range(NC):
                for m in range(DF):
                    act.wait_ge(s["z_ready"], c * DF + m + 1)
                    e.activation(hidden[:, m, c * CH:(c + 1) * CH], ps_z(m, c), ACT.Silu,
                                 bias=b1[:, m:m + 1]).then_inc(s["hidden_ready"], 1)
            act.wait_ge(s["lw_ready"], 1)
            e.activation(lmwo_mix[:, :], ps_lw, ACT.Copy).then_inc(s["lw_taken"], 1)
            act.wait_ge(s["pe_ready"], 1)
            e.activation(pub_exp[:, :], ps_pe, ACT.Copy).then_inc(s["pe_taken"], 1)
            for t in range(NT):
                t0, n = tokens(t)
                act.wait_ge(s["xt_ready"], t + 1)
                e.activation(xT[:, 0, t0:t0 + n], ps_xt(t, 0)[:, 0:n], ACT.Copy,
                             scale=w_in[:, 0:1]).then_inc(s["xt_act"], 1)
                if t == 1:
                    act.wait_ge(s["bus_ready"], 1)
                    e.activation(bus_w[:, :, :], ps_bus, ACT.Copy).then_inc(s["bus_taken"], 1)
            for c in range(NC):
                act.wait_ge(s["qk_ready"], c + 1)
                e.activation(qs[:, c * CH:(c + 1) * CH], ps_qk[c][0:2 * DH, :], ACT.Copy,
                             scale=float(DH) ** -0.5).then_inc(s["q_taken"], 1)
            act.wait_ge(s["v_ready"], 1)
            e.activation(vs[:, :, :].rearrange("p j d -> p (j d)"), ps_v, ACT.Copy).then_inc(s["v_taken"], 1)
            act.wait_ge(s["r_ready"], 1)
            e.activation(rhid[:, :], ps_r, ACT.Silu, scale=1.0 / S).then_inc(s["rhid_ready"], 1)
            for i in range(2):
                act.wait_ge(s["sh_ready"], i + 1)
                e.activation(se[:, i, :, :], sh[:, i, :, :], ACT.Exp).then_inc(s["se_ready"], 1)
            act.wait_ge(s["lg_shift"], 1)
            e.activation(lge[:, :, :], lg[:, :, :], ACT.Exp).then_inc(s["lg_exp"], 1)
            act.wait_ge(s["arcb_ready"], 1)
            e.activation(arc_e[:, :], ps_arc, ACT.Exp, bias=arc_b[:, :], scale=float(D) ** -0.5,
                         accum_out=arc_s[:, :]).then_inc(s["arce_ready"], 1)
            act.wait_ge(s["pt_ready"], 1)
            e.activation(probs_t[:, 0:NPAIR // 2, :].rearrange("k j (i q) -> k j i q", i=2),
                         ps_pt[0].rearrange("k j (i q) -> k j i q", i=2)[:, :, :, 0:S],
                         ACT.Copy).then_inc(s["pt_act"], 1)
            for t in range(NT):
                _, n = tokens(t)
                act.wait_ge(s["o_ready"], t + 1)
                if t >= 1:
                    act.wait_ge(s["ssq_ready"], t)
                e.activation(sqj[0:n, :], ps_o(t)[0:n, :], ACT.Square,
                             accum_out=ssq[0:n, t:t + 1]).then_inc(s["ssq_ready"], 1)
            for t in range(NT):
                t0, n = tokens(t)
                act.wait_ge(s["yt_ready"], t + 1)
                e.activation(fT[:, :, t0:t0 + n], ps_yt(t)[:, :, 0:n], ACT.Copy).then_inc(s["ft_act"], 1)
            for i in range(NC * MF):
                act.wait_ge(s["fc_ready"], i + 1)
                if i >= 2:
                    act.wait_ge(s["hid2_ready"], i - 1)
                e.activation(relu[:, i % 2, :], ps_f(i), ACT.Relu).then_inc(s["relu_ready"], 1)

        @block.tensor
        def _(pe):
            mm = nc.tensor.matmul
            for k in range(KP):
                pe.wait_ge(pw_in[k], 16)
                for c in range(NC):
                    for m in range(DF):
                        last = mm(ps_z(m, c), pw[:, k, T + m * P:T + (m + 1) * P],
                                  pw[:, k, c * CH:(c + 1) * CH], start=(k == 0), stop=(k == KP - 1))
                        if k == KP - 1:
                            last.then_inc(s["z_ready"], 1)
            pe.wait_ge(s["a_in"], 16)
            for t in range(NT):
                t0, n = tokens(t)
                pe.wait_ge(s["hidden_ready"], DF * (1 if t0 + n <= CH else 2))
                if t >= 2:
                    pe.wait_ge(s["h0_ready"], t - 1)
                for k in range(DF):
                    last = mm(ps_h(t)[0:n, :], hidden[:, k, t0:t0 + n], w2[:, k, :],
                              start=(k == 0), stop=(k == DF - 1))
                last.then_inc(s["h_ready"], 1)
            pe.wait_ge(s["b_in"], 16)
            pe.wait_ge(s["c_in"], 16)
            for k in range(DF):
                last = mm(ps_lw, lmwo[:, k, :], mix[:, k, :], start=(k == 0), stop=(k == DF - 1))
            last.then_inc(s["lw_ready"], 1)
            mm(ps_pe, publish_t, expand, start=True, stop=True).then_inc(s["pe_ready"], 1)
            pe.wait_ge(const_ready, 3)

            def transposes(out, in_, n):
                for f in range(DF):
                    last = nc.tensor.transpose(out(f)[:, 0:n], in_[0:n, f * P:(f + 1) * P], ident[0:n, 0:n])
                return last

            for t in range(NT):
                t0, n = tokens(t)
                pe.wait_ge(s["xhat_ready"], t + 1)
                if t >= 2:
                    pe.wait_ge(s["xt_act"], t - 1)
                    pe.wait_ge(s["xt_dve"], t - 1)
                transposes(lambda f: ps_xt(t, f), xhat[:, t, :], n).then_inc(s["xt_ready"], 1)
                if t == 0:
                    pe.wait_ge(s["lw_taken"], 1)
                    pe.wait_ge(s["pe_taken"], 1)
                    for f in range(DF):
                        last = mm(ps_bus[:, f, :], compress_t[:, f * P:(f + 1) * P], pub_exp[:, :],
                                  start=True, stop=True)
                    last.then_inc(s["bus_ready"], 1)
            for c in range(NC):
                pe.wait_ge(s["xt_act"], tiles_before((c + 1) * CH))
                pe.wait_ge(s["xt_dve"], tiles_before((c + 1) * CH))
                for k in range(DF):
                    last = mm(ps_qk[c], wqk[:, k, :], xT[:, k, c * CH:(c + 1) * CH],
                              start=(k == 0), stop=(k == DF - 1))
                last.then_inc(s["qk_ready"], 1)
            for j in range(NPAIR):
                for k in range(DF):
                    last = mm(ps_v[:, j * DH:(j + 1) * DH], xT[:, k, j * PAIR:(j + 1) * PAIR], wv[:, k, :],
                              start=(k == 0), stop=(k == DF - 1))
            last.then_inc(s["v_ready"], 1)
            pe.wait_ge(s["pad_ready"], 3)
            pe.wait_ge(s["bus_taken"], 1)
            pe.wait_ge(s["q_taken"], NC)
            pe.wait_ge(s["k_taken"], NC)
            for i in range(2):
                for b in range(B):
                    row = HALF * (b % 2)
                    last = mm(ps_s[i][row:row + HALF, b // 2, :],
                              qs[i * DH:(i + 1) * DH, b * S:b * S + HALF],
                              ks[i * DH:(i + 1) * DH, b * S:(b + 1) * S], start=True, stop=True)
                last.then_inc(s["s_ready"], 1)
            pe.wait_ge(s["route_ready"], DF)
            for k in range(DF):
                last = mm(ps_r, rw1[:, k, :], route[:, k, :], start=(k == 0), stop=(k == DF - 1))
            last.then_inc(s["r_ready"], 1)
            for k in range(DF):
                last = mm(ps_arc, xT[:, k, S - 1:T:S], lmwo[:, k, 0:SLOTS], start=(k == 0), stop=(k == DF - 1))
            last.then_inc(s["arc_ready"], 1)
            pe.wait_ge(s["rhid_ready"], 1)
            pe.wait_ge(s["rw2b_ready"], 3)
            for j in range(3):
                last = mm(ps_lg[:, j, :], rw2_b[:, j, :], rhid[:, :], start=True, stop=True)
            last.then_inc(s["lg_ready"], 1)
            pe.wait_ge(s["probs_ready"], 2)
            pe.wait_ge(s["v_taken"], 1)
            for i in range(2):
                for j in range(NPAIR // 2):
                    last = nc.tensor.transpose(ps_pt[i][:, j, :], probs[:, i * NPAIR // 2 + j, :], ident[:, :])
                last.then_inc(s["pt_ready"], 1)
            pe.wait_ge(s["arcp_ready"], 1)
            nc.tensor.transpose(ps_arct, arc_p[:, :], ident[0:B, 0:B]).then_inc(s["arct_ready"], 1)
            pe.wait_ge(s["v_taken"], 1)
            for i in range(2):
                pe.wait_ge(s["pt_act"] if i == 0 else s["pt_dve"], 1)
                for jj in range(NPAIR // 2):
                    j = i * NPAIR // 2 + jj
                    last = mm(ps_c[i][:, jj * PAIR:(jj + 1) * PAIR], vs[:, j, :], probs_t[:, j, :],
                              start=True, stop=True)
                last.then_inc(s["c_ready"], 1)
            pe.wait_ge(s["ssm_ready"], DF)
            pe.wait_ge(s["mixs_ready"], DF)
            for t in range(NT):
                t0, n = tokens(t)
                for k in range(DF):
                    mm(ps_o(t)[0:n, :], xT[:, k, t0:t0 + n], mix[:, DF + k, :], start=(k == 0), stop=False)
                for k in range(DF):
                    mm(ps_o(t)[0:n, :], ssm[:, k, t0:t0 + n], mix_ssm[:, k, :], start=False, stop=False)
                if t == 0:
                    pe.wait_ge(s["c_taken"], 2)
                    pe.wait_ge(s["arc_taken"], 1)
                mm(ps_o(t)[0:n, :], comb[:, t0:t0 + n], lmwo_mix[:, :],
                   start=False, stop=True).then_inc(s["o_ready"], 1)
            for t in range(NT):
                _, n = tokens(t)
                pe.wait_ge(s["out2_ready"], t + 1)
                for f in range(DF):
                    last = mm(ps_m[f], out2[0:n, t, f * P:(f + 1) * P], image_mean[0:n, t, :],
                              start=(t == 0), stop=(t == NT - 1))
            last.then_inc(s["m_ready"], 1)
            pe.wait_ge(s["meanb_ready"], DF)
            mean_t = mean_b[:, :, :, :].rearrange("p f b s -> p f (b s)")
            for t in range(NT):
                t0, n = tokens(t)
                for k in range(DF):
                    last = mm(ps_x(t)[0:n, :], mean_t[:, k, t0:t0 + n], bus_w[:, k, :],
                              start=(k == 0), stop=(k == DF - 1))
                last.then_inc(s["x_ready"], 1)
            for t in range(NT):
                t0, n = tokens(t)
                pe.wait_ge(s["yhat_ready"], t + 1)
                if t >= 3:
                    pe.wait_ge(s["ft_act"], t - 2)
                transposes(lambda f: ps_yt(t)[:, f, :], yhat[:, t, :], n).then_inc(s["yt_ready"], 1)
            pe.wait_ge(s["f_in"], 16)
            for c in range(NC):
                pe.wait_ge(s["ft_act"], tiles_before((c + 1) * CH))
                for m in range(MF):
                    i = c * MF + m
                    if i >= len(FC_BANKS):
                        pe.wait_ge(s["relu_ready"], i - len(FC_BANKS) + 1)
                    for k in range(DF):
                        last = mm(ps_f(i), wf[:, k, m * P:(m + 1) * P], fT[:, k, c * CH:(c + 1) * CH],
                                  start=(k == 0), stop=(k == DF - 1))
                    last.then_inc(s["fc_ready"], 1)
            pe.wait_ge(s["p_in"], 16)
            for t in range(NT):
                t0, n = tokens(t)
                pe.wait_ge(s["hid2_ready"], MF * (1 if t0 + n <= CH else 2))
                for m in range(MF):
                    last = mm(ps_y(t)[0:n, :], hid2[:, m, t0:t0 + n], wp[:, m, :],
                              start=(m == 0), stop=(m == MF - 1))
                last.then_inc(s["y_ready"], 1)

        @block.vector
        def _(dve):
            v = nc.vector

            def h0_stats(t):
                _, n = tokens(t)
                dve.wait_ge(s["h_ready"], t + 1)
                v.tensor_tensor(h0[0:n, t, :], ps_h(t)[0:n, :], b2[0:n, :], ALU.add).then_inc(s["h0_ready"], 1)
                dve.wait_ge(s["h0_ready"], t + 1)
                v.bn_stats(stats[0:n, t, :], h0[0:n, t, :]).then_inc(s["stats_ready"], 1)
                dve.wait_ge(s["stats_ready"], t + 1)
                v.bn_aggr(mv[0:n, t, :], stats[0:n, t, :]).then_inc(s["mv_ready"], 1)
                dve.wait_ge(s["mv_ready"], t + 1)
                v.tensor_scalar(ve[0:n, t, 0:1], mv[0:n, t, 1:2], EPS_LN, None, ALU.add)
                v.tensor_scalar(ve[0:n, t, 1:2], mv[0:n, t, 1:2], 1.0 + EPS_RMS, EPS_RMS * EPS_LN,
                                ALU.mult, ALU.add).then_inc(s["ve_ready"], 1)

            def make_xhat(t):
                _, n = tokens(t)
                dve.wait_ge(s["rs_ready"], t + 1)
                v.tensor_scalar(xhat[0:n, t, :], h0[0:n, t, :], mv[0:n, t, 0:1], rs[0:n, t, 1:2],
                                ALU.subtract, ALU.mult).then_inc(s["xhat_ready"], 1)

            def take_xt(t):
                t0, n = tokens(t)
                dve.wait_ge(s["xt_ready"], t + 1)
                v.tensor_scalar(xT[:, 1, t0:t0 + n], ps_xt(t, 1)[:, 0:n], w_in[:, 1:2], None,
                                ALU.mult).then_inc(s["xt_dve"], 1)

            dve.wait_ge(s["a_in"], 16)
            for i in range(NT + 2):
                if i < NT:
                    h0_stats(i)
                if 1 <= i <= NT:
                    make_xhat(i - 1)
                if i >= 2:
                    take_xt(i - 2)
            v.tensor_scalar(neg_lam[:, :], slr_lam, -1.0, None, ALU.mult).then_inc(s["neg_ready"], 1)
            for c in range(NC):
                dve.wait_ge(s["q_taken"], c + 1)
                v.tensor_copy(ks[:, c * CH:(c + 1) * CH], ps_qk[c][2 * DH:4 * DH, :]).then_inc(s["k_taken"], 1)
            dve.wait_ge(s["xt_act"], NT)
            dve.wait_ge(s["xt_dve"], NT)
            for f in range(DF):
                v.tensor_reduce(route[:, f, :], xT[:, f, :].rearrange("p (b s) -> p b s", s=S),
                                AX.X, ALU.add).then_inc(s["route_ready"], 1)
            for i in range(2):
                dve.wait_ge(s["s_ready"], i + 1)
                v.tensor_reduce(smax[:, i, :], ps_s[i], AX.X, ALU.max).then_inc(s["smax_ready"], 1)
                dve.wait_ge(s["smax_ready"], i + 1)
                v.tensor_tensor(sh[:, i, :, :], ps_s[i], smax[:, i, :].unsqueeze(2).to_broadcast([P, NPAIR, S]),
                                ALU.subtract).then_inc(s["sh_ready"], 1)
            dve.wait_ge(lam_prep, 2 * DF + 1)
            v.tensor_tensor_scan(ssm[:, 0, :], lam_scan[:, 0, :], xT[:, 0, :], 0.0, ALU.mult,
                                 ALU.add).then_inc(s["ssm_ready"], 1)
            for i in range(2):
                dve.wait_ge(s["se_ready"], i + 1)
                v.tensor_reduce(ssum[:, i, :], se[:, i, :, :], AX.X, ALU.add).then_inc(s["ssum_ready"], 1)
                dve.wait_ge(s["ssum_ready"], i + 1)
                v.reciprocal(srec[:, i, :], ssum[:, i, :]).then_inc(s["srec_ready"], 1)
            dve.wait_ge(s["srec_ready"], 2)
            dve.wait_ge(s["neg_ready"], 1)
            v.tensor_scalar(sfac[:, :], srec[:, 1, :], neg_lam[:, :], None, ALU.mult).then_inc(s["sfac_ready"], 1)
            v.tensor_tensor(sp[:, 0, :, :], se[:, 0, :, :], srec[:, 0, :].unsqueeze(2).to_broadcast([P, NPAIR, S]),
                            ALU.mult).then_inc(s["sp_ready"], 1)
            dve.wait_ge(s["sfac_ready"], 1)
            v.tensor_tensor(sp[:, 1, :, :], se[:, 1, :, :], sfac[:, :].unsqueeze(2).to_broadcast([P, NPAIR, S]),
                            ALU.mult).then_inc(s["sp_ready"], 1)
            dve.wait_ge(s["sp_ready"], 2)
            dve.wait_ge(s["pad_ready"], 3)
            for r in range(2):
                rows = slice(r * HALF, (r + 1) * HALF)
                v.tensor_tensor(probs[rows, :, r * S:(r + 1) * S], sp[rows, 0, :, :], sp[rows, 1, :, :],
                                ALU.add).then_inc(s["probs_ready"], 1)
            dve.wait_ge(s["lg_ready"], 1)
            v.tensor_tensor(lg[:, :, :], ps_lg.rearrange("p j b -> p b j"),
                            rb2.unsqueeze(1).to_broadcast([P, B, 3]), ALU.add).then_inc(s["lg_chain"], 1)
            dve.wait_ge(s["arc_ready"], 1)
            v.tensor_reduce(arc_m[:, :], ps_arc, AX.X, ALU.max).then_inc(s["arcm_ready"], 1)
            dve.wait_ge(s["lg_chain"], 1)
            v.tensor_reduce(lgm[:, :], lg[:, :, :], AX.X, ALU.max).then_inc(s["lg_chain"], 1)
            dve.wait_ge(s["arcm_ready"], 1)
            v.tensor_scalar(arc_b[:, :], arc_m[:, :], -float(D) ** -0.5, None, ALU.mult).then_inc(s["arcb_ready"], 1)
            dve.wait_ge(s["lg_chain"], 2)
            v.tensor_tensor(lg[:, :, :], lg[:, :, :], lgm[:, :].unsqueeze(2).to_broadcast([P, B, 3]),
                            ALU.subtract).then_inc(s["lg_shift"], 1)
            v.tensor_tensor_scan(ssm[:, 1, :], lam_scan[:, 1, :], xT[:, 1, :], 0.0, ALU.mult,
                                 ALU.add).then_inc(s["ssm_ready"], 1)
            dve.wait_ge(s["pt_ready"], 2)
            v.tensor_copy(probs_t[:, NPAIR // 2:NPAIR, :].rearrange("k j (i q) -> k j i q", i=2),
                          ps_pt[1].rearrange("k j (i q) -> k j i q", i=2)[:, :, :, 0:S]).then_inc(s["pt_dve"], 1)
            dve.wait_ge(s["lg_exp"], 1)
            v.tensor_reduce(lgs[:, :], lge[:, :, :], AX.X, ALU.add).then_inc(s["lg_chain"], 1)
            v.tensor_tensor(gsum[:, :], lge[:, :, 1], lge[:, :, 2], ALU.add).then_inc(s["lg_chain"], 1)
            dve.wait_ge(s["arce_ready"], 1)
            v.reciprocal(arc_r[:, :], arc_s[:, :]).then_inc(s["arcr_ready"], 1)
            dve.wait_ge(s["lg_chain"], 4)
            v.reciprocal(lgr[:, :], lgs[:, :]).then_inc(s["lg_chain"], 1)
            dve.wait_ge(s["arcr_ready"], 1)
            v.tensor_scalar(arc_p[:, :], arc_e[:, :], arc_r[:, :], None, ALU.mult).then_inc(s["arcp_ready"], 1)
            dve.wait_ge(s["lg_chain"], 5)
            v.tensor_tensor(gate[:, :], gsum[:, :], lgr[:, :], ALU.mult).then_inc(s["gate_ready"], 1)
            v.tensor_tensor(p_full[:, :], lge[:, :, 2], lgr[:, :], ALU.mult).then_inc(s["pfull_ready"], 1)
            dve.wait_ge(s["arct_ready"], 1)
            dve.wait_ge(s["pfull_ready"], 1)
            v.tensor_tensor(comb[0:SLOTS, S - 1:T:S], ps_arct, p_full[0:SLOTS, :],
                            ALU.mult).then_inc(s["arc_taken"], 1)
            dve.wait_ge(s["gate_ready"], 1)
            for c in range(NC):
                dve.wait_ge(s["c_ready"], c + 1)
                b0 = c * B // NC
                v.tensor_tensor(comb[SLOTS:SLOTS + DH, c * CH:(c + 1) * CH].rearrange("p (b s) -> p b s", s=S),
                                ps_c[c].rearrange("p (b s) -> p b s", s=S),
                                gate[SLOTS:SLOTS + DH, b0:b0 + B // NC].unsqueeze(2).to_broadcast([DH, B // NC, S]),
                                ALU.mult).then_inc(s["c_taken"], 1)

            def rms_factor(t):
                _, n = tokens(t)
                dve.wait_ge(s["ssq_ready"], t + 1)
                v.tensor_scalar(rve[0:n, t:t + 1], ssq[0:n, t:t + 1], 1.0 / D, EPS_RMS,
                                ALU.mult, ALU.add).then_inc(s["rve_ready"], 1)

            def mixer_out(t):
                _, n = tokens(t)
                dve.wait_ge(s["rr_ready"], t + 1)
                v.scalar_tensor_tensor(rms[0:n, t, :], ps_o(t)[0:n, :], rr[0:n, t:t + 1], w_out[0:n, :],
                                       ALU.mult, ALU.mult).then_inc(s["rms_ready"], 1)
                dve.wait_ge(s["rms_ready"], t + 1)
                dve.wait_ge(s["a_ready"], t + 1)
                v.tensor_tensor(out2[0:n, t, :], rms[0:n, t, :], a[0:n, t, :], ALU.add).then_inc(s["out2_ready"], 1)

            dve.wait_ge(s["b_in"], 16)
            for i in range(NT + 1):
                if i < NT:
                    rms_factor(i)
                if i >= 1:
                    mixer_out(i - 1)
            dve.wait_ge(s["m_ready"], 1)
            for f in range(DF):
                v.tensor_scalar(mean_b[:, f, :, :], ps_m[f].unsqueeze(2).to_broadcast([P, B, S]), 0.1, None,
                                ALU.mult).then_inc(s["meanb_ready"], 1)

            def h1_stats(t):
                _, n = tokens(t)
                dve.wait_ge(s["x_ready"], t + 1)
                dve.wait_ge(s["h1p_ready"], t + 1)
                v.tensor_tensor(h1[0:n, t, :], ps_x(t)[0:n, :], h1p[0:n, t, :], ALU.add).then_inc(s["h1_ready"], 1)
                dve.wait_ge(s["h1_ready"], t + 1)
                v.bn_stats(stats2[0:n, t, :], h1[0:n, t, :]).then_inc(s["stats2_ready"], 1)
                dve.wait_ge(s["stats2_ready"], t + 1)
                v.bn_aggr(mv2[0:n, t, :], stats2[0:n, t, :]).then_inc(s["mv2_ready"], 1)
                dve.wait_ge(s["mv2_ready"], t + 1)
                v.tensor_scalar(ve2[0:n, t:t + 1], mv2[0:n, t, 1:2], EPS_LN, None, ALU.add).then_inc(s["ve2_ready"], 1)

            def make_yhat(t):
                _, n = tokens(t)
                dve.wait_ge(s["rs2_ready"], t + 1)
                v.tensor_scalar(yhat[0:n, t, :], h1[0:n, t, :], mv2[0:n, t, 0:1], rs2[0:n, t:t + 1],
                                ALU.subtract, ALU.mult).then_inc(s["yhat_ready"], 1)

            for i in range(NT + 1):
                if i < NT:
                    h1_stats(i)
                if i >= 1:
                    make_yhat(i - 1)
            for i in range(NC * MF):
                c, m = divmod(i, MF)
                dve.wait_ge(s["relu_ready"], i + 1)
                v.tensor_tensor(hid2[:, m, c * CH:(c + 1) * CH], relu[:, i % 2, :], relu[:, i % 2, :],
                                ALU.mult).then_inc(s["hid2_ready"], 1)
            for t in range(NT):
                _, n = tokens(t)
                dve.wait_ge(s["y_ready"], t + 1)
                v.tensor_scalar(count[0:n, t, 0, :], ps_y(t)[0:n, :], thresholds[0], None,
                                ALU.is_gt).then_inc(s["count_ready"], 1)
                for j in range(1, NUM_STEPS):
                    dve.wait_ge(s["count_ready"], NUM_STEPS * t + j)
                    v.scalar_tensor_tensor(count[0:n, t, j, :], ps_y(t)[0:n, :], thresholds[j],
                                           count[0:n, t, j - 1, :], ALU.is_gt, ALU.add).then_inc(s["count_ready"], 1)
                dve.wait_ge(s["count_ready"], NUM_STEPS * (t + 1))
                v.scalar_tensor_tensor(result[0:n, t, :], count[0:n, t, NUM_STEPS - 1, :], 1.0 / NUM_STEPS,
                                       h1[0:n, t, :], ALU.mult, ALU.add).then_inc(s["result_ready"], 1)


def lay_out(i):
    def chunks(w):
        w = np.asarray(w)
        return w.reshape(w.shape[0] // P, P, w.shape[1]).transpose(1, 0, 2)

    def flat(w):
        return chunks(w).reshape(P, -1)

    def rows(x, n):
        return np.broadcast_to(np.asarray(x).reshape(1, n), (P, n))

    x = np.asarray(i["x"]).reshape(B, 3, GRID, PATCH, GRID, PATCH)
    x = x.transpose(1, 3, 5, 0, 2, 4).reshape(KP * P, T)
    cols = [np.asarray(i[n]).reshape(DF, P).T for n in ("L0_tok_b1", "L0_attn_w_norm_in")]
    lam = np.repeat(np.asarray(i["L0_attn_lambdas"]), D // HEADS).reshape(DF, P).T
    qk = np.concatenate([np.asarray(i["L0_attn_slr_" + n]) for n in ("wq1", "wq2", "wk1", "wk2")], axis=1)
    lmwo = np.concatenate([np.asarray(i["L0_attn_landmarks"]), np.asarray(i["L0_attn_slr_wo"])], axis=0).T
    arrays = {
        "patches_w1": np.concatenate([chunks(x), chunks(i["L0_tok_W1"])], axis=2),
        "pack_a": np.concatenate([flat(i["L0_tok_W2"]), rows(i["L0_tok_b2"], D), *cols, lam,
                                  rows(i["L0_attn_router_b2"], 3), rows(i["L0_attn_slr_lam"], 1)], axis=1),
        "pack_b": np.concatenate([flat(qk), flat(i["L0_attn_slr_wv"]), flat(i["L0_attn_router_w1"]), flat(lmwo),
                                  np.asarray(i["L0_attn_router_w2"]), rows(i["L0_attn_w_norm_out"], D)], axis=1),
        "pack_c": np.concatenate([flat(i["L0_attn_mix_w"]), np.asarray(i["L0_attn_bus_compress"]).T,
                                  np.asarray(i["L0_attn_bus_publish"]).T, np.asarray(i["L0_attn_bus_expand"])], axis=1),
        "w_fc": chunks(np.asarray(i["L0_ffn_W_fc"]).T),
        "w_proj": chunks(np.asarray(i["L0_ffn_W_proj"]).T),
    }
    return {n: np.ascontiguousarray(v) for n, v in arrays.items()}


def kernel(**inputs):
    import concourse.bacc as bacc
    from concourse.bass_utils import run_bass_kernel_spmd

    nc = bacc.Bacc("TRN2", target_bir_lowering=False, num_devices=1)
    arrays = {n + "_dram": v for n, v in lay_out(inputs).items()}
    args = [nc.dram_tensor(n, v.shape, mybir.dt.from_np(v.dtype), kind="ExternalInput").ap()
            for n, v in arrays.items()]
    out = nc.dram_tensor("out_dram", (T, D), F32, kind="ExternalOutput").ap()
    build(nc, *args, out)
    r = run_bass_kernel_spmd(nc, [arrays], core_ids=[0])
    return r.results[0]["out_dram"].reshape(B, S, D)
```

```python
from contextlib import ExitStack

import numpy as np

import concourse.bass as bass
from concourse import mybir

ALU = mybir.AluOpType
ACT = mybir.ActivationFunctionType
F32 = mybir.dt.float32
F32R = mybir.dt.float32r
AX = mybir.AxisListType

P = 128
D = 256
DF = D // P
B = 16
GRID = 6
S = GRID * GRID
T = B * S
PATCH = 16
KP = 3 * PATCH * PATCH // P
DH = 32
SLOTS = 64
BUS = 128
F = 1024
MF = F // P
PAIR = 2 * S
NPAIR = B // 2
HALF = 64
HEADS = 8
EPS_LN = 1e-5
EPS_RMS = 1.1920929e-07
BETA, THRESHOLD, NUM_STEPS = 0.9, 1.0, 5

G_IMAGES = (10, 6)
G_TILES = (3, 2)
G_FIRST = (0, G_IMAGES[0])
G_TOKENS = tuple(n * S for n in G_IMAGES)
G_AT = (0, G_TOKENS[0])
NG = len(G_IMAGES)
NB = max(G_IMAGES)
NT = sum(G_TILES)
GT = max(G_TOKENS)
TILES = [(g, G_AT[g] + j * (G_TOKENS[g] // G_TILES[g]), G_TOKENS[g] // G_TILES[g])
         for g in range(NG) for j in range(G_TILES[g])]
TILES_OF = [[t for t, tile in enumerate(TILES) if tile[0] == g] for g in range(NG)]
PAIRS_OF = [range(G_FIRST[g] // 2, (G_FIRST[g] + G_IMAGES[g]) // 2) for g in range(NG)]
NBUF = 3
FILL = (8, 4, 2, 2)
WARM = 10
WC = 512

W2_AT, B2_AT = 0, DF * D
PACK_A = B2_AT + D
VEC = 3 * DF + 3 + 1
QK_AT = 0
V_AT = QK_AT + DF * P
R1_AT = V_AT + DF * DH
LW_AT = R1_AT + DF * P
R2_AT = LW_AT + DF * (SLOTS + DH)
WO_AT = R2_AT + 3
PACK_B = WO_AT + D
BUS_AT = 2 * DF * D
PACK_C = BUS_AT + D + BUS + D
PACK_F = DF * F
PACK_P = MF * D


def group_span(g):
    return slice(G_AT[g], G_AT[g] + G_TOKENS[g])


def spike_thresholds():
    f = np.float32

    def count(y):
        mem, spikes = f(0), 0
        for _ in range(NUM_STEPS):
            reset = f(mem - f(THRESHOLD) > 0)
            mem = f(f(f(BETA) * mem) + y) - reset * f(THRESHOLD)
            spikes += int(mem - f(THRESHOLD) > 0)
        return spikes

    steps = []
    for n in range(1, NUM_STEPS + 1):
        low, high = f(0), f(2 * THRESHOLD)
        while np.nextafter(low, high) < high:
            mid = f((low + high) / 2)
            if count(mid) >= n:
                high = mid
            else:
                low = mid
        steps.append(float(low))
    return steps


def build(nc, v_d, pw0_d, pw1_d, a_d, b_d, c_d, f_d, p_d, out_d):
    thresholds = spike_thresholds()
    ctx = ExitStack()
    with ctx:
        def sb(name, shape, dtype=F32):
            return ctx.enter_context(nc.sbuf_tensor(name, shape, dtype))

        def sem(name):
            return ctx.enter_context(nc.semaphore(name))

        W0 = D + G_TOKENS[0]
        PW = KP * (D + T)
        pw = sb("patches_and_w1", [P, PW])
        pw_hi = sb("pw_hi", [P, PW], F32R)
        pw_lo = sb("pw_lo", [P, PW], F32R)

        def w1_of(x, k, m):
            return x[:, k * W0 + m * P:k * W0 + (m + 1) * P]

        def patches_of(x, k, g):
            at = k * W0 + D if g == 0 else KP * W0 + k * G_TOKENS[1]
            return x[:, at:at + G_TOKENS[g]]

        hid_hi = pw_hi[:, 0:MF * T].rearrange("p (m n) -> p m n", m=MF)
        hid_lo = pw_lo[:, 0:MF * T].rearrange("p (m n) -> p m n", m=MF)

        vec = sb("vectors", [P, VEC])
        wa = sb("pack_a", [P, PACK_A])
        wb = sb("pack_b", [P, PACK_B])
        wc = sb("pack_c", [P, PACK_C])
        wf = pw[:, 0:DF * F]
        wp = pw[:, DF * F:DF * F + MF * D]
        wf_hi, wf_lo = sb("wf_hi", [P, DF * F], F32R), sb("wf_lo", [P, DF * F], F32R)
        wp_hi, wp_lo = sb("wp_hi", [P, MF * D], F32R), sb("wp_lo", [P, MF * D], F32R)
        w2 = wa[:, W2_AT:B2_AT].rearrange("p (k n) -> p k n", k=DF)
        b2 = wa[:, B2_AT:PACK_A]
        b1, w_in, lam = vec[:, 0:2], vec[:, 2:4], vec[:, 4:6]
        rb2, slr_lam = vec[:, 6:9], vec[:, 9:10]
        wqk = wb[:, QK_AT:V_AT].rearrange("p (k n) -> p k n", k=DF)
        wv = wb[:, V_AT:R1_AT].rearrange("p (k n) -> p k n", k=DF)
        rw1 = wb[:, R1_AT:LW_AT].rearrange("p (k n) -> p k n", k=DF)
        lmwo = wb[:, LW_AT:R2_AT].rearrange("p (k n) -> p k n", k=DF)
        rw2 = wb[:, R2_AT:WO_AT]
        w_out = wb[:, WO_AT:PACK_B]
        mix = wc[:, 0:BUS_AT].rearrange("p (k n) -> p k n", k=2 * DF)
        compress_t = wc[:, BUS_AT:BUS_AT + D]
        publish_t = wc[:, BUS_AT + D:BUS_AT + D + BUS]
        expand = wc[:, BUS_AT + D + BUS:PACK_C]

        ident = sb("ident", [P, P])
        image_sum = sb("image_sum", [P, NT, B])
        image_row = sb("image_row", [NB, GT])
        minus_half = sb("minus_half", [P, 2])
        warm = sb("warm", [P, 512], mybir.dt.bfloat16)
        loaded = sb("loaded", [P, 2])
        var_scale = sb("var_scale", [P, 2])
        var_shift = sb("var_shift", [P, 2])
        lam_scan = sb("lam_scan", [P, DF, GT])
        one_minus_lam = sb("one_minus_lam", [P, DF])
        mix_ssm = sb("mix_ssm", [P, DF, D])
        rw2_b = sb("rw2_b", [P, 3, P])
        neg_lam = sb("neg_lam", [P, 1])

        hidden = sb("hidden", [P, DF, T])
        h0 = sb("h0", [P, NT, D])
        stats = sb("stats", [P, NT, 6])
        mv = sb("mv", [P, NT, 2])
        ve = sb("ve", [P, NT, 2])
        rs = sb("rs", [P, NT, 2])
        nm = sb("nm", [P, NT, 2])
        xhat = sb("xhat", [P, NT, D])
        xT = sb("xT", [P, DF, T])
        a = sb("a", [P, NT, D])
        out2 = sb("out2", [P, NT, D])
        lmwo_mix = sb("lmwo_mix", [SLOTS + DH, D])
        pub_exp = sb("pub_exp", [BUS, D])
        bus_w = sb("bus_w", [P, DF, D])
        Q_AT = [G_AT[g] + g * (HALF - S) for g in range(NG)]
        qs = sb("qs", [2 * DH, T + NG * (HALF - S)])
        ks = sb("ks", [2 * DH, T])
        vs = sb("vs", [PAIR, NPAIR, DH])
        route = sb("route", [P, DF, B])
        rhid, rexp, rden, rrec = (sb(n, [P, B]) for n in ("rhid", "rexp", "rden", "rrec"))
        lg = sb("lg", [P, B, 3])
        lgm = sb("lgm", [P, B])
        lgd = sb("lgd", [P, B, 3])
        lge = sb("lge", [P, B, 3])
        lgs = sb("lgs", [P, B])
        lgr = sb("lgr", [P, B])
        gate = sb("gate", [P, B])
        gsum = sb("gsum", [P, B])
        p_full = sb("p_full", [P, B])
        smax = sb("smax", [P, 2, NPAIR])
        sh = sb("sh", [P, 2, NPAIR, S])
        se = sb("se", [P, 2, NPAIR, S])
        ssum = sb("ssum", [P, 2, NPAIR])
        srec = sb("srec", [P, 2, NPAIR])
        sfac = sb("sfac", [P, NPAIR])
        sp = sb("sp", [P, 2, NPAIR, S])
        probs = sb("probs", [P, NPAIR, PAIR])
        probs_t = sb("probs_t", [PAIR, NPAIR, PAIR])
        arc_m = sb("arc_m", [B, 1])
        arc_b = sb("arc_b", [B, 1])
        arc_e = sb("arc_e", [B, SLOTS])
        arc_s = sb("arc_s", [B, 1])
        arc_r = sb("arc_r", [B, 1])
        arc_p = sb("arc_p", [B, SLOTS])
        comb = sb("comb", [SLOTS + DH, T])
        ssm = sb("ssm", [P, DF, T])
        sqj = sb("sqj", [P, D])
        ssq = sb("ssq", [P, NT])
        rve = sb("rve", [P, NT])
        rr = sb("rr", [P, NT])
        rms = sb("rms", [P, NT, D])
        h1p = sb("h1p", [P, NT, D])
        mean = sb("mean", [P, NG, DF, NB])
        row = sb("row", [NB, NG, D])
        h1 = h1p
        stats2 = sb("stats2", [P, NT, 6])
        mv2 = sb("mv2", [P, NT, 2])
        ve2 = sb("ve2", [P, NT])
        rs2 = sb("rs2", [P, NT])
        yhat = rms
        f_hi, f_lo = sb("f_hi", [P, DF, T], F32R), sb("f_lo", [P, DF, T], F32R)
        relu = sb("relu", [P, NBUF, GT])
        square = sb("square", [P, NBUF, GT])
        count, result = xhat, a

        bank = [ctx.enter_context(nc.psum_tensor(f"bank{i}", [P, 512], F32)) for i in range(8)]

        def ps_z(g, m):
            return bank[2 * g + m][:, 0:G_TOKENS[g]]

        XT_BANKS = [6, 0, 6, 2, 2]

        def ps_h(t):
            return bank[4 + t % 2][:, 0:D]

        def ps_xt(t, f):
            return bank[XT_BANKS[t] + f][:, 0:P]

        ps_qk = [bank[0][:, 0:n] for n in G_TOKENS]
        ps_v = [bank[1][0:PAIR, 0:len(js) * DH] for js in PAIRS_OF]
        ps_lw = bank[4][0:SLOTS + DH, 0:D]
        ps_pe = bank[5][:, 0:D]
        ps_bus = bank[4][:, :].rearrange("p (f n) -> p f n", f=DF)

        def ps_s(g, i):
            n = len(PAIRS_OF[g])
            return bank[6 + i][:, 0:n * S].rearrange("p (j k) -> p j k", j=n)

        ps_r = bank[5][:, 0:DF * B].rearrange("p (f b) -> p f b", f=DF)
        ps_hid = bank[5][:, 64:64 + B]
        ps_lg = bank[5][:, 128:128 + 3 * B].rearrange("p (j b) -> p j b", j=3)
        ps_arc = bank[4][0:B, 0:SLOTS]
        ps_arct = bank[4][0:SLOTS, 64:64 + B]

        PT = [[(0, PAIRS_OF[0][0:3]), (1, PAIRS_OF[0][3:])], [(1, PAIRS_OF[1])]]

        def ps_pt(b, n):
            return bank[b][0:PAIR, 0:n * P].rearrange("p (j q) -> p j q", j=n)

        def ps_c(g):
            return bank[(7, 4)[g]][SLOTS:SLOTS + DH, 0:G_TOKENS[g]]

        O_AT = [(2, 0), (2, D), (3, 0), (6, 0), (6, D)]
        X_BANKS = [2, 0, 3, 6, 7]
        YT_BANKS = [1, 4, 7, 1, 4]
        FC_BANKS = [0, 2, 3]
        Y_BANKS = [6, 7, 1, 4, 5]

        def ps_o(t):
            b_, at = O_AT[t]
            return bank[b_][:, at:at + D]

        def ps_x(t):
            return bank[X_BANKS[t]][:, 0:D]

        def ps_m(g, f):
            return bank[5][:, f * NB:f * NB + G_IMAGES[g]]

        def ps_row(g):
            return bank[5][0:G_IMAGES[g], D:2 * D]

        def ps_yt(t):
            return bank[YT_BANKS[t]][:, 0:D].rearrange("p (f n) -> p f n", f=DF)

        def ps_f(i):
            return bank[FC_BANKS[i % len(FC_BANKS)]][:, 0:G_TOKENS[i // MF]]

        def ps_y(t):
            return bank[Y_BANKS[t]][:, 0:D]

        names = """v_in warm_ready out2_ready row_ready row_taken a_in b_in c_in f_in p_in const_zero const_ready pad_ready lam_ready mixs_ready
        rw2b_ready w1lo_ready pwhi_ready pwlo_ready wfhi_ready wflo_ready wphi_ready wplo_ready
        z_ready hidden_ready h_ready h0_ready stats_ready mv_ready ve_ready rs_ready nm_ready
        xhat_ready a_ready xt_ready xt_act xt_dve lw_ready pe_ready bus_ready lw_taken
        pe_taken bus_taken qk_ready q_taken k_taken v_ready v_taken route_ready r_ready
        rexp_ready rden_ready rrec_ready rhid_ready lg_ready lg_added lg_max lg_shift lg_exp lg_sum lg_gsum lg_rec gate_ready
        pfull_ready s_ready smax_ready sh_ready se_ready ssum_ready srec_ready sfac_ready neg_ready
        sp_ready probs_ready pt_ready pt_taken c_ready c_taken arc_ready arcm_ready arcb_ready
        arce_ready arcr_ready arcp_ready arct_ready arc_taken ssm_ready o_ready ssq_ready rve_ready
        rr_ready rms_ready h1p_ready m_ready mean_ready x_ready h1_ready
        stats2_ready mv2_ready ve2_ready rs2_ready yhat_ready yt_ready fhi_ready flo_ready fc_ready
        relu_ready square_ready hidhi_ready hidlo_pool hidlo_dve y_ready count_ready result_ready
        out_sem""".split()
        s = {n: sem(n) for n in names}
        pw0_in = [sem(f"pw0_in{k}") for k in range(KP)]
        pw1_in = [sem(f"pw1_in{h}") for h in range(2)]
        K1 = KP // 2
        G1 = KP * W0

        def by_pool(n):
            return n - n // 3

        block = ctx.enter_context(nc.Block())

        @block.sync
        def _(sp_):
            for k in range(KP):
                sp_.dma_start(pw[:, k * W0:(k + 1) * W0], pw0_d[:, k * W0:(k + 1) * W0]).then_inc(pw0_in[k], 16)
            n = K1 * G_TOKENS[1]
            for h in range(2):
                sp_.dma_start(pw[:, G1 + h * n:G1 + (h + 1) * n], pw1_d[:, h * n:(h + 1) * n]).then_inc(pw1_in[h], 16)
                if h == 0:
                    sp_.dma_start(wa[:, :], a_d).then_inc(s["a_in"], 16)
            sp_.dma_start(wb[:, :], b_d).then_inc(s["b_in"], 16)
            sp_.dma_start(wc[:, :], c_d).then_inc(s["c_in"], 16)
            sp_.wait_ge(s["w1lo_ready"], KP)
            sp_.wait_ge(s["pwlo_ready"], KP + 2)
            sp_.dma_start(wf[:, :], f_d).then_inc(s["f_in"], 16)
            sp_.dma_start(wp[:, :], p_d).then_inc(s["p_in"], 16)
            for t, (_, t0, n) in enumerate(TILES):
                sp_.wait_ge(s["result_ready"], t + 1)
                sp_.dma_start(out_d[t0:t0 + n, :], result[0:n, t, :]).then_inc(s["out_sem"], 16)
            sp_.wait_ge(s["out_sem"], 16 * NT)

        @block.gpsimd
        def _(pool):
            g_ = nc.gpsimd
            g_.memset(warm[:, :], 0.5).then_inc(s["warm_ready"], 1)
            g_.memset(loaded[:, :], 0.0).then_inc(s["warm_ready"], 1)
            for k in range(KP):
                pool.wait_ge(s["pwhi_ready"], k + 1)
                g_.tensor_tensor(pw_lo[:, k * W0:k * W0 + D], pw[:, k * W0:k * W0 + D],
                                 pw_hi[:, k * W0:k * W0 + D].bitcast(F32), ALU.subtract).then_inc(s["w1lo_ready"], 1)
            g_.memset(ident[:, :], 0.0).then_inc(s["const_zero"], 1)
            g_.memset(image_sum[:, :, :], 1.0).then_inc(s["const_zero"], 1)
            g_.memset(image_row[:, :], 1.0).then_inc(s["const_zero"], 1)
            g_.memset(minus_half[:, :], -0.5).then_inc(s["const_ready"], 1)
            g_.memset(var_scale[:, 0:1], 1.0).then_inc(s["const_ready"], 1)
            g_.memset(var_scale[:, 1:2], 1.0 + EPS_RMS).then_inc(s["const_ready"], 1)
            g_.memset(var_shift[:, 0:1], EPS_LN).then_inc(s["const_ready"], 1)
            g_.memset(var_shift[:, 1:2], EPS_RMS * EPS_LN).then_inc(s["const_ready"], 1)
            pool.wait_ge(s["const_zero"], 3)
            g_.affine_select(out=ident[:, :], in_=ident[:, :], compare_op=ALU.not_equal, fill=1.0,
                             base=0, pattern=[[-1, P]], channel_multiplier=1).then_inc(s["const_ready"], 1)
            for g in range(NG):
                t_, n_ = TILES_OF[g][0], TILES[TILES_OF[g][0]][2]
                part = image_sum[:, t_:t_ + G_TILES[g], :]
                g_.affine_select(out=part, in_=part, compare_op=ALU.is_ge, fill=0.0, base=G_AT[g],
                                 pattern=[[n_, G_TILES[g]], [-S, B]],
                                 channel_multiplier=1).then_inc(s["const_zero"], 1)
            g_.affine_select(out=image_row[:, :], in_=image_row[:, :], compare_op=ALU.is_ge, fill=0.0,
                             base=0, pattern=[[1, GT]], channel_multiplier=-S).then_inc(s["const_zero"], 1)
            pool.wait_ge(s["const_zero"], 6)
            for g in range(NG):
                t_, n_ = TILES_OF[g][0], TILES[TILES_OF[g][0]][2]
                part = image_sum[:, t_:t_ + G_TILES[g], :]
                g_.affine_select(out=part, in_=part, compare_op=ALU.is_ge, fill=0.0, base=S - 1 - G_AT[g],
                                 pattern=[[-n_, G_TILES[g]], [S, B]],
                                 channel_multiplier=-1).then_inc(s["const_ready"], 1)
            g_.affine_select(out=image_row[:, :], in_=image_row[:, :], compare_op=ALU.is_ge, fill=0.0,
                             base=S - 1, pattern=[[-1, GT]], channel_multiplier=S).then_inc(s["const_ready"], 1)
            g_.memset(probs[:, :, :], 0.0).then_inc(s["pad_ready"], 1)
            g_.memset(comb[0:SLOTS, :], 0.0).then_inc(s["pad_ready"], 1)
            for g in range(NG):
                at = Q_AT[g] + G_TOKENS[g]
                g_.memset(qs[:, at:at + HALF - S], 0.0).then_inc(s["pad_ready"], 1)
            def ln_power(t):
                n = TILES[t][2]
                pool.wait_ge(s["ve_ready"], t + 1)
                g_.tensor_tensor(rs[0:n, t, :], ve[0:n, t, :], minus_half[0:n, :], ALU.pow).then_inc(s["rs_ready"], 1)

            def rms_power(t):
                n = TILES[t][2]
                pool.wait_ge(s["rve_ready"], t + 1)
                g_.tensor_tensor(rr[0:n, t:t + 1], rve[0:n, t:t + 1], minus_half[0:n, 0:1],
                                 ALU.pow).then_inc(s["rr_ready"], 1)

            def add_residual(t):
                n = TILES[t][2]
                pool.wait_ge(s["out2_ready"], t + 1)
                g_.tensor_tensor(h1p[0:n, t, :], out2[0:n, t, :], h0[0:n, t, :], ALU.add).then_inc(s["h1p_ready"], 1)

            def ln2_power(t):
                n = TILES[t][2]
                pool.wait_ge(s["ve2_ready"], t + 1)
                g_.tensor_tensor(rs2[0:n, t:t + 1], ve2[0:n, t:t + 1], minus_half[0:n, 0:1],
                                 ALU.pow).then_inc(s["rs2_ready"], 1)

            def low_part(w, hi, lo, c, hi_ready, lo_ready):
                pool.wait_ge(hi_ready, c + 1)
                at = slice(c * WC, (c + 1) * WC)
                g_.tensor_tensor(lo[:, at], w[:, at], hi[:, at].bitcast(F32), ALU.subtract).then_inc(lo_ready, 1)

            def wf_low(c):
                low_part(wf, wf_hi, wf_lo, c, s["wfhi_ready"], s["wflo_ready"])

            def wp_low(c):
                low_part(wp, wp_hi, wp_lo, c, s["wphi_ready"], s["wplo_ready"])

            def hid_low(i):
                g, m = divmod(i, MF)
                pool.wait_ge(s["square_ready"], i + 1)
                pool.wait_ge(s["hidhi_ready"], i + 1)
                g_.tensor_tensor(hid_lo[:, m, group_span(g)], square[:, i % NBUF, 0:G_TOKENS[g]],
                                 hid_hi[:, m, group_span(g)].bitcast(F32),
                                 ALU.subtract).then_inc(s["hidlo_pool"], 1)

            for t in TILES_OF[0]:
                ln_power(t)
            pool.wait_ge(s["v_in"], 16)
            for f in range(DF):
                g_.tensor_copy(lam_scan[:, f, :], lam[:, f:f + 1].to_broadcast([P, GT])).then_inc(s["lam_ready"], 1)
            pool.wait_ge(s["lam_ready"], DF)
            for f in range(DF):
                g_.memset(lam_scan[:, f, :].rearrange("p (b s) -> p b s", s=S)[:, :, 0:1],
                          0.0).then_inc(s["lam_ready"], 1)
            g_.tensor_scalar(one_minus_lam[:, :], lam, -1.0, 1.0, ALU.mult, ALU.add).then_inc(s["lam_ready"], 1)
            for t in TILES_OF[1]:
                ln_power(t)
            pool.wait_ge(s["b_in"], 16)
            for j in range(3):
                g_.tensor_copy(rw2_b[:, j, :], rw2[:, j:j + 1].to_broadcast([P, P])).then_inc(s["rw2b_ready"], 1)
            pool.wait_ge(s["c_in"], 16)
            pool.wait_ge(s["lam_ready"], 2 * DF + 1)
            for f in range(DF):
                g_.tensor_scalar(mix_ssm[:, f, :], mix[:, f, :], one_minus_lam[:, f:f + 1], None,
                                 ALU.mult).then_inc(s["mixs_ready"], 1)
            for c in range(DF * F // WC):
                wf_low(c)
            for t in TILES_OF[0]:
                rms_power(t)
            for t in TILES_OF[0]:
                add_residual(t)
            for c in range(3):
                wp_low(c)
            rms_power(3)
            rms_power(4)
            ln2_power(0)
            ln2_power(1)
            ln2_power(2)
            wp_low(3)
            add_residual(3)
            add_residual(4)
            for t in TILES_OF[1]:
                ln2_power(t)
            for i in range(NG * MF):
                if i % 3 != 2:
                    hid_low(i)

        @block.scalar
        def _(act):
            e = nc.scalar
            act.dma_start(vec[:, :], v_d).then_inc(s["v_in"], 16)
            act.wait_ge(s["warm_ready"], 2)
            e.activation(loaded[:, 0:1], loaded[:, 1:2], ACT.Silu)
            for k in range(KP):
                act.wait_ge(pw0_in[k], 16)
                e.activation(pw_hi[:, k * W0:(k + 1) * W0], pw[:, k * W0:(k + 1) * W0],
                             ACT.Copy).then_inc(s["pwhi_ready"], 1)
            n1 = K1 * G_TOKENS[1]
            for h in range(2):
                act.wait_ge(pw1_in[h], 16)
                e.activation(pw_hi[:, G1 + h * n1:G1 + (h + 1) * n1], pw[:, G1 + h * n1:G1 + (h + 1) * n1],
                             ACT.Copy).then_inc(s["pwhi_ready"], 1)

            def silu(g):
                for m in range(DF):
                    act.wait_ge(s["z_ready"], g * DF + m + 1)
                    e.activation(hidden[:, m, group_span(g)], ps_z(g, m), ACT.Silu,
                                 bias=b1[:, m:m + 1]).then_inc(s["hidden_ready"], 1)

            def normed(t):
                n = TILES[t][2]
                act.wait_ge(s["nm_ready"], t + 1)
                e.activation(xhat[0:n, t, :], h0[0:n, t, :], ACT.Identity, bias=nm[0:n, t, 1:2],
                             scale=rs[0:n, t, 1:2]).then_inc(s["xhat_ready"], 1)

            def layernorm(t):
                n = TILES[t][2]
                e.activation(a[0:n, t, :], h0[0:n, t, :], ACT.Identity, bias=nm[0:n, t, 0:1],
                             scale=rs[0:n, t, 0:1]).then_inc(s["a_ready"], 1)

            def take_xt(t):
                _, t0, n = TILES[t]
                act.wait_ge(s["xt_ready"], t + 1)
                e.activation(xT[:, 0, t0:t0 + n], ps_xt(t, 0)[:, 0:n], ACT.Copy,
                             scale=w_in[:, 0:1]).then_inc(s["xt_act"], 1)

            def take_q(g):
                act.wait_ge(s["qk_ready"], g + 1)
                e.activation(qs[:, Q_AT[g]:Q_AT[g] + G_TOKENS[g]], ps_qk[g][0:2 * DH, :], ACT.Copy,
                             scale=float(DH) ** -0.5).then_inc(s["q_taken"], 1)

            def take_v(g):
                act.wait_ge(s["v_ready"], g + 1)
                j0, n = PAIRS_OF[g][0], len(PAIRS_OF[g])
                e.activation(vs[:, j0:j0 + n, :].rearrange("p j d -> p (j d)"), ps_v[g],
                             ACT.Copy).then_inc(s["v_taken"], 1)

            def router_hidden():
                act.wait_ge(s["r_ready"], 1)
                e.activation(rexp[:, :], ps_hid, ACT.Exp, scale=-1.0 / S).then_inc(s["rexp_ready"], 1)

            def exps(g):
                j0, n = PAIRS_OF[g][0], len(PAIRS_OF[g])
                act.wait_ge(s["sh_ready"], g + 1)
                e.activation(se[:, :, j0:j0 + n, :], sh[:, :, j0:j0 + n, :], ACT.Exp).then_inc(s["se_ready"], 1)

            def exp_router():
                act.wait_ge(s["lg_shift"], 1)
                e.activation(lge[:, :, :], lgd[:, :, :], ACT.Exp).then_inc(s["lg_exp"], 1)

            def exp_arc():
                act.wait_ge(s["arcb_ready"], 1)
                e.activation(arc_e[:, :], ps_arc, ACT.Exp, bias=arc_b[:, :],
                             scale=float(D) ** -0.5, accum_out=arc_s[:, :]).then_inc(s["arce_ready"], 1)

            def take_probs(n_, g, part):
                act.wait_ge(s["pt_ready"], n_ + 1)
                b_, js = PT[g][part]
                e.activation(probs_t[:, js[0]:js[0] + len(js), :].rearrange("k j (i q) -> k j i q", i=2),
                             ps_pt(b_, len(js)).rearrange("k j (i q) -> k j i q", i=2)[:, :, :, 0:S],
                             ACT.Copy).then_inc(s["pt_taken"], 1)

            def squares(t):
                n = TILES[t][2]
                act.wait_ge(s["o_ready"], [1, 1, 2, 3, 3][t])
                if t >= 1:
                    act.wait_ge(s["ssq_ready"], t)
                e.activation(sqj[0:n, :], ps_o(t)[0:n, :], ACT.Square, scale=float(D) ** -0.5,
                             accum_out=ssq[0:n, t:t + 1]).then_inc(s["ssq_ready"], 1)

            def take_row(g):
                nb = G_IMAGES[g]
                act.wait_ge(s["row_ready"], g + 1)
                e.activation(row[0:nb, g, :], ps_row(g), ACT.Copy).then_inc(s["row_taken"], 1)

            def f_high(t):
                _, t0, n = TILES[t]
                act.wait_ge(s["yt_ready"], t + 1)
                e.activation(f_hi[:, :, t0:t0 + n], ps_yt(t)[:, :, 0:n], ACT.Copy).then_inc(s["fhi_ready"], 1)

            def high_part(w, hi, c, ready):
                at = slice(c * WC, (c + 1) * WC)
                e.activation(hi[:, at], w[:, at], ACT.Copy).then_inc(ready, 1)

            def relu_of(i):
                g = i // MF
                act.wait_ge(s["fc_ready"], i + 1)
                if i >= NBUF:
                    act.wait_ge(s["square_ready"], i - NBUF + 1)
                e.activation(relu[:, i % NBUF, 0:G_TOKENS[g]], ps_f(i), ACT.Relu).then_inc(s["relu_ready"], 1)

            def hid_high(i):
                g, m = divmod(i, MF)
                act.wait_ge(s["relu_ready"], i + 1)
                e.activation(hid_hi[:, m, group_span(g)], relu[:, i % NBUF, 0:G_TOKENS[g]],
                             ACT.Square).then_inc(s["hidhi_ready"], 1)

            act.wait_ge(s["v_in"], 16)
            silu(0)
            normed(0)
            normed(1)
            silu(1)
            normed(2)
            for t in TILES_OF[0]:
                take_xt(t)
            e.activation(loaded[:, 0:1], loaded[:, 1:2], ACT.Exp)
            take_q(0)
            normed(3)
            take_v(0)
            normed(4)
            take_xt(3)
            take_xt(4)
            exps(0)
            act.wait_ge(s["lw_ready"], 1)
            e.activation(lmwo_mix[:, :], ps_lw, ACT.Copy).then_inc(s["lw_taken"], 1)
            act.wait_ge(s["pe_ready"], 1)
            e.activation(pub_exp[:, :], ps_pe, ACT.Copy).then_inc(s["pe_taken"], 1)
            take_q(1)
            take_v(1)
            act.wait_ge(s["bus_ready"], 1)
            e.activation(bus_w[:, :, :], ps_bus, ACT.Copy).then_inc(s["bus_taken"], 1)
            act.wait_ge(s["f_in"], 16)
            high_part(wf, wf_hi, 0, s["wfhi_ready"])
            take_probs(0, 0, 0)
            take_probs(1, 0, 1)
            high_part(wf, wf_hi, 1, s["wfhi_ready"])
            router_hidden()
            exps(1)
            high_part(wf, wf_hi, 2, s["wfhi_ready"])
            exp_arc()
            exp_router()
            layernorm(0)
            high_part(wf, wf_hi, 3, s["wfhi_ready"])
            act.wait_ge(s["p_in"], 16)
            layernorm(1)
            layernorm(2)
            for t in TILES_OF[0]:
                squares(t)
            take_probs(2, 1, 0)
            layernorm(3)
            layernorm(4)
            for c in range(MF * D // WC):
                high_part(wp, wp_hi, c, s["wphi_ready"])
            take_row(0)
            squares(3)
            squares(4)
            f_high(0)
            f_high(1)
            f_high(2)
            relu_of(0)
            take_row(1)
            hid_high(0)
            for i in range(1, NG * MF):
                relu_of(i)
                hid_high(i)
                if i == 3:
                    f_high(3)
                    f_high(4)

        @block.tensor
        def _(pe):
            mm = nc.tensor.matmul

            def mm_split(out, left, right, start, stop):
                mm(out, left[0], right[1], start=start, stop=False)
                mm(out, left[1], right[0], start=False, stop=False)
                return mm(out, left[0], right[0], start=False, stop=stop)

            def keep_warm(b_, n):
                for _ in range(n):
                    mm(bank[b_][:, :], warm[:, 0:P], warm[:, :], start=True, stop=True)

            def tokenizer_up(g, ks):
                for k in ks:
                    if g == 0:
                        pe.wait_ge(s["pwhi_ready"], k + 1)
                        pe.wait_ge(s["w1lo_ready"], k + 1)
                        pe.wait_ge(s["pwlo_ready"], k + 1)
                    elif k % K1 == 0:
                        pe.wait_ge(s["pwhi_ready"], KP + k // K1 + 1)
                        pe.wait_ge(s["pwlo_ready"], KP + k // K1 + 1)
                    for m in range(DF):
                        last = mm_split(ps_z(g, m), (w1_of(pw_hi, k, m), w1_of(pw_lo, k, m)),
                                        (patches_of(pw_hi, k, g), patches_of(pw_lo, k, g)),
                                        start=(k == 0), stop=(k == KP - 1))
                        if k == KP - 1:
                            last.then_inc(s["z_ready"], 1)

            def tokenizer_down(t):
                g, t0, n = TILES[t]
                pe.wait_ge(s["hidden_ready"], DF * (g + 1))
                if t >= 2:
                    pe.wait_ge(s["h0_ready"], t - 1)
                for k in range(DF):
                    last = mm(ps_h(t)[0:n, :], hidden[:, k, t0:t0 + n], w2[:, k, :],
                              start=(k == 0), stop=(k == DF - 1))
                last.then_inc(s["h_ready"], 1)

            def transposes(out, in_, n):
                for f in range(DF):
                    last = nc.tensor.transpose(out(f)[:, 0:n], in_[0:n, f * P:(f + 1) * P], ident[0:n, 0:n])
                return last

            def transpose_x(t):
                n = TILES[t][2]
                pe.wait_ge(s["xhat_ready"], t + 1)
                before = [None, None, 1, None, 4][t]
                if before:
                    pe.wait_ge(s["xt_act"], before)
                    pe.wait_ge(s["xt_dve"], before)
                transposes(lambda f: ps_xt(t, f), xhat[:, t, :], n).then_inc(s["xt_ready"], 1)

            def queries_keys(g):
                pe.wait_ge(s["xt_act"], TILES_OF[g][-1] + 1)
                pe.wait_ge(s["xt_dve"], TILES_OF[g][-1] + 1)
                if g >= 1:
                    pe.wait_ge(s["q_taken"], g)
                    pe.wait_ge(s["k_taken"], g)
                for k in range(DF):
                    last = mm(ps_qk[g], wqk[:, k, :], xT[:, k, group_span(g)],
                              start=(k == 0), stop=(k == DF - 1))
                last.then_inc(s["qk_ready"], 1)

            def values(g):
                if g >= 1:
                    pe.wait_ge(s["v_taken"], g)
                for jj, j in enumerate(PAIRS_OF[g]):
                    for k in range(DF):
                        last = mm(ps_v[g][:, jj * DH:(jj + 1) * DH], xT[:, k, j * PAIR:(j + 1) * PAIR],
                                  wv[:, k, :], start=(k == 0), stop=(k == DF - 1))
                last.then_inc(s["v_ready"], 1)

            def scores(g):
                pe.wait_ge(s["q_taken"], g + 1)
                pe.wait_ge(s["k_taken"], g + 1)
                if g >= 1:
                    pe.wait_ge(s["sh_ready"], g)
                q0 = Q_AT[g] - G_AT[g]
                for i in range(2):
                    for b in range(G_FIRST[g], G_FIRST[g] + G_IMAGES[g]):
                        row = HALF * (b % 2)
                        last = mm(ps_s(g, i)[row:row + HALF, (b - G_FIRST[g]) // 2, :],
                                  qs[i * DH:(i + 1) * DH, q0 + b * S:q0 + b * S + HALF],
                                  ks[i * DH:(i + 1) * DH, b * S:(b + 1) * S], start=True, stop=True)
                    last.then_inc(s["s_ready"], 1)

            def router_up():
                pe.wait_ge(s["route_ready"], 1)
                for k in range(DF):
                    last = mm(ps_hid, rw1[:, k, :], route[:, k, :], start=(k == 0), stop=(k == DF - 1))
                last.then_inc(s["r_ready"], 1)

            def router_logits():
                pe.wait_ge(s["rhid_ready"], 1)
                pe.wait_ge(s["rw2b_ready"], 3)
                for j in range(3):
                    last = mm(ps_lg[:, j, :], rw2_b[:, j, :], rhid[:, :], start=True, stop=True)
                last.then_inc(s["lg_ready"], 1)

            def arc_logits():
                for k in range(DF):
                    last = mm(ps_arc, xT[:, k, S - 1:T:S], lmwo[:, k, 0:SLOTS],
                              start=(k == 0), stop=(k == DF - 1))
                last.then_inc(s["arc_ready"], 1)

            def arc_transpose():
                pe.wait_ge(s["arcp_ready"], 1)
                nc.tensor.transpose(ps_arct, arc_p[:, :], ident[0:B, 0:B]).then_inc(s["arct_ready"], 1)

            def transpose_probs(g):
                pe.wait_ge(s["probs_ready"], 2 * (g + 1))
                if g == 0:
                    pe.wait_ge(s["q_taken"], NG)
                    pe.wait_ge(s["k_taken"], NG)
                    pe.wait_ge(s["v_taken"], NG)
                else:
                    pe.wait_ge(s["pt_taken"], len(PT[0]))
                for b_, js in PT[g]:
                    for jj, j in enumerate(js):
                        last = nc.tensor.transpose(ps_pt(b_, len(js))[:, jj, :], probs[:, j, :], ident[:, :])
                    last.then_inc(s["pt_ready"], 1)

            def context(g):
                pe.wait_ge(s["v_taken"], g + 1)
                pe.wait_ge(s["pt_taken"], len(PT[0]) if g == 0 else len(PT[0]) + len(PT[1]))
                for jj, j in enumerate(PAIRS_OF[g]):
                    last = mm(ps_c(g)[:, jj * PAIR:(jj + 1) * PAIR], vs[:, j, :], probs_t[:, j, :],
                              start=True, stop=True)
                last.then_inc(s["c_ready"], 1)

            def mixer(g, part, tiles=None):
                if part == 1:
                    pe.wait_ge(s["mixs_ready"], DF)
                    pe.wait_ge(s["ssm_ready"], DF * (g + 1))
                for t in tiles or TILES_OF[g]:
                    _, t0, n = TILES[t]
                    for k in range(DF):
                        left, right = (xT, mix[:, DF + k, :]) if part == 0 else (ssm, mix_ssm[:, k, :])
                        mm(ps_o(t)[0:n, :], left[:, k, t0:t0 + n], right,
                           start=(part == 0 and k == 0 and O_AT[t][1] == 0), stop=False,
                           skip_group_check=True)

            def mixer_end(g):
                pe.wait_ge(s["c_taken"], g + 1)
                pe.wait_ge(s["arc_taken"], 1)
                for t in TILES_OF[g]:
                    _, t0, n = TILES[t]
                    last = mm(ps_o(t)[0:n, :], comb[:, t0:t0 + n], lmwo_mix[:, :],
                              start=False, stop=True, skip_group_check=True)
                    if t + 1 == NT or O_AT[t + 1][0] != O_AT[t][0]:
                        last.then_inc(s["o_ready"], 1)

            def image_means(g, tiles=None):
                for t in tiles or TILES_OF[g]:
                    pe.wait_ge(s["out2_ready"], t + 1)
                    for f in range(DF):
                        n = TILES[t][2]
                        last = mm(ps_m(g, f), out2[0:n, t, f * P:(f + 1) * P],
                                  image_sum[0:n, t, G_FIRST[g]:G_FIRST[g] + G_IMAGES[g]],
                                  start=(t == TILES_OF[g][0] and f == 0), stop=(t == TILES_OF[g][-1]),
                                  skip_group_check=True)
                if t == TILES_OF[g][-1]:
                    last.then_inc(s["m_ready"], 1)

            def bus_rows(g):
                pe.wait_ge(s["mean_ready"], g + 1)
                for k in range(DF):
                    last = mm(ps_row(g), mean[:, g, k, 0:G_IMAGES[g]], bus_w[:, k, :],
                              start=(k == 0), stop=(k == DF - 1))
                last.then_inc(s["row_ready"], 1)

            def bus_spread(g):
                nb = G_IMAGES[g]
                pe.wait_ge(s["row_taken"], g + 1)
                for t in TILES_OF[g]:
                    _, t0, n = TILES[t]
                    at = t0 - G_AT[g]
                    mm(ps_x(t)[0:n, :], image_row[0:nb, at:at + n], row[0:nb, g, :],
                       start=True, stop=True).then_inc(s["x_ready"], 1)

            def transpose_y(t):
                n = TILES[t][2]
                pe.wait_ge(s["yhat_ready"], t + 1)
                before = [None, None, None, 1, 2][t]
                if before:
                    pe.wait_ge(s["flo_ready"], before)
                transposes(lambda f: ps_yt(t)[:, f, :], yhat[:, t, :], n).then_inc(s["yt_ready"], 1)

            def mlp_up(i):
                g, m = divmod(i, MF)
                if m == 0:
                    pe.wait_ge(s["fhi_ready"], TILES_OF[g][-1] + 1)
                    pe.wait_ge(s["flo_ready"], TILES_OF[g][-1] + 1)
                if i >= len(FC_BANKS):
                    pe.wait_ge(s["relu_ready"], i - len(FC_BANKS) + 1)
                for k in range(DF):
                    at = slice(k * F + m * P, k * F + (m + 1) * P)
                    last = mm_split(ps_f(i), (wf_hi[:, at], wf_lo[:, at]),
                                    (f_hi[:, k, group_span(g)], f_lo[:, k, group_span(g)]),
                                    start=(k == 0), stop=(k == DF - 1))
                last.then_inc(s["fc_ready"], 1)

            def mlp_down(t):
                g, t0, n = TILES[t]
                for m in range(MF):
                    if t == TILES_OF[g][0]:
                        i = MF * g + m
                        if i % 3 == 2:
                            pe.wait_ge(s["hidlo_dve"], (i + 1) // 3)
                        else:
                            pe.wait_ge(s["hidlo_pool"], by_pool(i + 1))
                    if m * D % WC == 0 and t == 0:
                        pe.wait_ge(s["wplo_ready"], m * D // WC + 1)
                    at = slice(m * D, (m + 1) * D)
                    last = mm_split(ps_y(t)[0:n, :], (hid_hi[:, m, t0:t0 + n], hid_lo[:, m, t0:t0 + n]),
                                    (wp_hi[:, at], wp_lo[:, at]), start=(m == 0), stop=(m == MF - 1))
                last.then_inc(s["y_ready"], 1)

            pe.wait_ge(s["warm_ready"], 1)
            keep_warm(7, WARM)
            tokenizer_up(0, range(KP))
            tokenizer_up(1, range(2))
            pe.wait_ge(s["a_in"], 16)
            for t in TILES_OF[0]:
                tokenizer_down(t)
            tokenizer_up(1, range(2, KP))
            pe.wait_ge(s["const_ready"], 9)
            transpose_x(0)
            transpose_x(1)
            tokenizer_down(3)
            transpose_x(2)
            tokenizer_down(4)
            pe.wait_ge(s["b_in"], 16)
            queries_keys(0)
            values(0)
            transpose_x(3)
            pe.wait_ge(s["pad_ready"], 2 + NG)
            scores(0)
            transpose_x(4)
            pe.wait_ge(s["h0_ready"], NT)
            pe.wait_ge(s["c_in"], 16)
            for k in range(DF):
                last = mm(ps_lw, lmwo[:, k, :], mix[:, k, :], start=(k == 0), stop=(k == DF - 1))
            last.then_inc(s["lw_ready"], 1)
            mm(ps_pe, publish_t, expand, start=True, stop=True).then_inc(s["pe_ready"], 1)
            queries_keys(1)
            values(1)
            pe.wait_ge(s["lw_taken"], 1)
            pe.wait_ge(s["pe_taken"], 1)
            for f in range(DF):
                last = mm(ps_bus[:, f, :], compress_t[:, f * P:(f + 1) * P], pub_exp[:, :],
                          start=True, stop=True)
            last.then_inc(s["bus_ready"], 1)
            mixer(0, 0, [0])
            transpose_probs(0)
            scores(1)
            pe.wait_ge(s["bus_taken"], 1)
            arc_logits()
            mixer(0, 0, [1])
            router_up()
            mixer(0, 0, [2])
            router_logits()
            mixer(0, 1, [0, 1])
            pe.wait_ge(s["sh_ready"], 2)
            context(0)
            mixer(0, 1, [2])
            arc_transpose()
            mixer_end(0)
            mixer(1, 0)
            transpose_probs(1)
            mixer(1, 1)
            pe.wait_ge(s["lg_added"], 1)
            image_means(0)
            context(1)
            bus_rows(0)
            mixer_end(1)
            bus_spread(0)
            keep_warm(7, FILL[0])
            transpose_y(0)
            transpose_y(1)
            keep_warm(0, FILL[1])
            transpose_y(2)
            keep_warm(2, FILL[2])
            image_means(1)
            keep_warm(2, FILL[3])
            pe.wait_ge(s["wflo_ready"], DF * F // WC)
            for i in range(MF):
                mlp_up(i)
                if i == 0:
                    bus_rows(1)
                if i == 1:
                    bus_spread(1)
                if i == 4:
                    transpose_y(3)
                    transpose_y(4)
            for i in range(MF, 2 * MF):
                mlp_up(i)
            for t in range(NT):
                mlp_down(t)

        @block.vector
        def _(dve):
            v = nc.vector
            for k in range(KP):
                dve.wait_ge(s["pwhi_ready"], k + 1)
                at = slice(k * W0 + D, (k + 1) * W0)
                v.tensor_tensor(pw_lo[:, at], pw[:, at], pw_hi[:, at].bitcast(F32),
                                ALU.subtract).then_inc(s["pwlo_ready"], 1)
            n1 = K1 * G_TOKENS[1]
            for h in range(2):
                dve.wait_ge(s["pwhi_ready"], KP + h + 1)
                at = slice(G1 + h * n1, G1 + (h + 1) * n1)
                v.tensor_tensor(pw_lo[:, at], pw[:, at], pw_hi[:, at].bitcast(F32),
                                ALU.subtract).then_inc(s["pwlo_ready"], 1)

            def h0_add(t):
                n = TILES[t][2]
                dve.wait_ge(s["h_ready"], t + 1)
                v.tensor_tensor(h0[0:n, t, :], ps_h(t)[0:n, :], b2[0:n, :], ALU.add).then_inc(s["h0_ready"], 1)

            def h0_stats(t):
                n = TILES[t][2]
                dve.wait_ge(s["h0_ready"], t + 1)
                v.bn_stats(stats[0:n, t, :], h0[0:n, t, :]).then_inc(s["stats_ready"], 1)

            def h0_moments(t):
                n = TILES[t][2]
                dve.wait_ge(s["stats_ready"], t + 1)
                v.bn_aggr(mv[0:n, t, :], stats[0:n, t, :]).then_inc(s["mv_ready"], 1)

            def h0_var(t):
                n = TILES[t][2]
                dve.wait_ge(s["mv_ready"], t + 1)
                v.scalar_tensor_tensor(ve[0:n, t, :], var_scale[0:n, :], mv[0:n, t, 1:2], var_shift[0:n, :],
                                       ALU.mult, ALU.add).then_inc(s["ve_ready"], 1)

            def neg_mean(t):
                n = TILES[t][2]
                dve.wait_ge(s["rs_ready"], t + 1)
                v.tensor_scalar(nm[0:n, t, :], rs[0:n, t, :], mv[0:n, t, 0:1], -1.0,
                                ALU.mult, ALU.mult).then_inc(s["nm_ready"], 1)

            def take_xt(t):
                _, t0, n = TILES[t]
                dve.wait_ge(s["xt_ready"], t + 1)
                v.tensor_scalar(xT[:, 1, t0:t0 + n], ps_xt(t, 1)[:, 0:n], w_in[:, 1:2], None,
                                ALU.mult).then_inc(s["xt_dve"], 1)

            def take_k(g):
                dve.wait_ge(s["qk_ready"], g + 1)
                v.tensor_copy(ks[:, group_span(g)], ps_qk[g][2 * DH:4 * DH, :]).then_inc(s["k_taken"], 1)

            def route_of():
                for f in range(DF):
                    last = v.tensor_reduce(route[:, f, :], xT[:, f, :].rearrange("p (b s) -> p b s", s=S),
                                           AX.X, ALU.add)
                last.then_inc(s["route_ready"], 1)

            def shift_scores(g):
                j0, n = PAIRS_OF[g][0], len(PAIRS_OF[g])
                for i in range(2):
                    dve.wait_ge(s["s_ready"], 2 * g + i + 1)
                    v.tensor_reduce(smax[:, i, j0:j0 + n], ps_s(g, i), AX.X, ALU.max).then_inc(s["smax_ready"], 1)
                for i in range(2):
                    dve.wait_ge(s["smax_ready"], 2 * g + i + 1)
                    last = v.tensor_tensor(sh[:, i, j0:j0 + n, :], ps_s(g, i),
                                           smax[:, i, j0:j0 + n].unsqueeze(2).to_broadcast([P, n, S]),
                                           ALU.subtract)
                last.then_inc(s["sh_ready"], 1)

            def scan(g, f):
                v.tensor_tensor_scan(ssm[:, f, group_span(g)], lam_scan[:, f, 0:G_TOKENS[g]],
                                     xT[:, f, group_span(g)], 0.0, ALU.mult, ALU.add).then_inc(s["ssm_ready"], 1)

            def make_probs(g):
                j0, n = PAIRS_OF[g][0], len(PAIRS_OF[g])
                dve.wait_ge(s["se_ready"], g + 1)
                v.tensor_reduce(ssum[:, :, j0:j0 + n], se[:, :, j0:j0 + n, :], AX.X, ALU.add).then_inc(s["ssum_ready"], 1)
                dve.wait_ge(s["ssum_ready"], g + 1)
                v.reciprocal(srec[:, :, j0:j0 + n], ssum[:, :, j0:j0 + n]).then_inc(s["srec_ready"], 1)
                dve.wait_ge(s["srec_ready"], g + 1)
                v.tensor_scalar(sfac[:, j0:j0 + n], srec[:, 1, j0:j0 + n], neg_lam[:, :], None,
                                ALU.mult).then_inc(s["sfac_ready"], 1)
                v.tensor_tensor(sp[:, 0, j0:j0 + n, :], se[:, 0, j0:j0 + n, :],
                                srec[:, 0, j0:j0 + n].unsqueeze(2).to_broadcast([P, n, S]),
                                ALU.mult).then_inc(s["sp_ready"], 1)
                dve.wait_ge(s["sfac_ready"], g + 1)
                v.tensor_tensor(sp[:, 1, j0:j0 + n, :], se[:, 1, j0:j0 + n, :],
                                sfac[:, j0:j0 + n].unsqueeze(2).to_broadcast([P, n, S]),
                                ALU.mult).then_inc(s["sp_ready"], 1)
                dve.wait_ge(s["sp_ready"], 2 * (g + 1))
                for r in range(2):
                    rows = slice(r * HALF, (r + 1) * HALF)
                    v.tensor_tensor(probs[rows, j0:j0 + n, r * S:(r + 1) * S], sp[rows, 0, j0:j0 + n, :],
                                    sp[rows, 1, j0:j0 + n, :], ALU.add).then_inc(s["probs_ready"], 1)

            def router_hidden():
                dve.wait_ge(s["rexp_ready"], 1)
                v.tensor_scalar(rden[:, :], rexp[:, :], 1.0, None, ALU.add).then_inc(s["rden_ready"], 1)
                dve.wait_ge(s["rden_ready"], 1)
                v.reciprocal(rrec[:, :], rden[:, :]).then_inc(s["rrec_ready"], 1)
                dve.wait_ge(s["rrec_ready"], 1)
                v.scalar_tensor_tensor(rhid[:, :], ps_hid, 1.0 / S, rrec[:, :],
                                       ALU.mult, ALU.mult).then_inc(s["rhid_ready"], 1)

            def router_shift():
                dve.wait_ge(s["lg_ready"], 1)
                v.tensor_tensor(lg[:, :, :], ps_lg.rearrange("p j b -> p b j"),
                                rb2.unsqueeze(1).to_broadcast([P, B, 3]), ALU.add).then_inc(s["lg_added"], 1)
                dve.wait_ge(s["lg_added"], 1)
                v.tensor_reduce(lgm[:, :], lg[:, :, :], AX.X, ALU.max).then_inc(s["lg_max"], 1)
                dve.wait_ge(s["lg_max"], 1)
                v.tensor_tensor(lgd[:, :, :], lg[:, :, :], lgm[:, :].unsqueeze(2).to_broadcast([P, B, 3]),
                                ALU.subtract).then_inc(s["lg_shift"], 1)

            def router_gates():
                dve.wait_ge(s["lg_exp"], 1)
                v.tensor_reduce(lgs[:, :], lge[:, :, :], AX.X, ALU.add).then_inc(s["lg_sum"], 1)
                v.tensor_tensor(gsum[:, :], lge[:, :, 1], lge[:, :, 2], ALU.add).then_inc(s["lg_gsum"], 1)
                dve.wait_ge(s["lg_sum"], 1)
                v.reciprocal(lgr[:, :], lgs[:, :]).then_inc(s["lg_rec"], 1)
                dve.wait_ge(s["lg_rec"], 1)
                dve.wait_ge(s["lg_gsum"], 1)
                v.tensor_tensor(gate[:, :], gsum[:, :], lgr[:, :], ALU.mult).then_inc(s["gate_ready"], 1)
                v.tensor_tensor(p_full[:, :], lge[:, :, 2], lgr[:, :], ALU.mult).then_inc(s["pfull_ready"], 1)

            def arc_shift():
                dve.wait_ge(s["arc_ready"], 1)
                v.tensor_reduce(arc_m[:, :], ps_arc, AX.X, ALU.max).then_inc(s["arcm_ready"], 1)
                dve.wait_ge(s["arcm_ready"], 1)
                v.tensor_scalar(arc_b[:, :], arc_m[:, :], -float(D) ** -0.5, None,
                                ALU.mult).then_inc(s["arcb_ready"], 1)

            def arc_probs():
                dve.wait_ge(s["arce_ready"], 1)
                v.reciprocal(arc_r[:, :], arc_s[:, :]).then_inc(s["arcr_ready"], 1)
                dve.wait_ge(s["arcr_ready"], 1)
                v.tensor_scalar(arc_p[:, :], arc_e[:, :], arc_r[:, :], None,
                                ALU.mult).then_inc(s["arcp_ready"], 1)

            def gated_arc():
                dve.wait_ge(s["arct_ready"], 1)
                dve.wait_ge(s["pfull_ready"], 1)
                v.tensor_tensor(comb[0:SLOTS, S - 1:T:S], ps_arct, p_full[0:SLOTS, :],
                                ALU.mult).then_inc(s["arc_taken"], 1)

            def gated_context(g):
                b0, nb = G_FIRST[g], G_IMAGES[g]
                dve.wait_ge(s["gate_ready"], 1)
                dve.wait_ge(s["c_ready"], g + 1)
                v.tensor_tensor(comb[SLOTS:SLOTS + DH, group_span(g)].rearrange("p (b s) -> p b s", s=S),
                                ps_c(g).rearrange("p (b s) -> p b s", s=S),
                                gate[SLOTS:SLOTS + DH, b0:b0 + nb].unsqueeze(2).to_broadcast([DH, nb, S]),
                                ALU.mult).then_inc(s["c_taken"], 1)

            def rms_arg(t):
                n = TILES[t][2]
                dve.wait_ge(s["ssq_ready"], t + 1)
                v.tensor_scalar(rve[0:n, t:t + 1], ssq[0:n, t:t + 1], EPS_RMS, None,
                                ALU.add).then_inc(s["rve_ready"], 1)

            def mixer_out(t):
                n = TILES[t][2]
                dve.wait_ge(s["rr_ready"], t + 1)
                v.scalar_tensor_tensor(rms[0:n, t, :], ps_o(t)[0:n, :], rr[0:n, t:t + 1], w_out[0:n, :],
                                       ALU.mult, ALU.mult).then_inc(s["rms_ready"], 1)

            def mixer_add(t):
                n = TILES[t][2]
                dve.wait_ge(s["rms_ready"], t + 1)
                dve.wait_ge(s["a_ready"], t + 1)
                v.tensor_tensor(out2[0:n, t, :], rms[0:n, t, :], a[0:n, t, :], ALU.add).then_inc(s["out2_ready"], 1)

            def take_mean(g):
                nb = G_IMAGES[g]
                dve.wait_ge(s["m_ready"], g + 1)
                v.tensor_scalar(mean[:, g, :, 0:nb],
                                bank[5][:, 0:DF * NB].rearrange("p (f b) -> p f b", f=DF)[:, :, 0:nb],
                                1.0 / S, 0.1, ALU.mult, ALU.mult).then_inc(s["mean_ready"], 1)

            def h1_add(t):
                n = TILES[t][2]
                dve.wait_ge(s["x_ready"], t + 1)
                dve.wait_ge(s["h1p_ready"], t + 1)
                v.tensor_tensor(h1[0:n, t, :], ps_x(t)[0:n, :], h1p[0:n, t, :], ALU.add).then_inc(s["h1_ready"], 1)

            def h1_stats(t):
                n = TILES[t][2]
                dve.wait_ge(s["h1_ready"], t + 1)
                v.bn_stats(stats2[0:n, t, :], h1[0:n, t, :]).then_inc(s["stats2_ready"], 1)

            def h1_moments(t):
                n = TILES[t][2]
                dve.wait_ge(s["stats2_ready"], t + 1)
                v.bn_aggr(mv2[0:n, t, :], stats2[0:n, t, :]).then_inc(s["mv2_ready"], 1)

            def h1_var(t):
                n = TILES[t][2]
                dve.wait_ge(s["mv2_ready"], t + 1)
                v.tensor_scalar(ve2[0:n, t:t + 1], mv2[0:n, t, 1:2], EPS_LN, None, ALU.add).then_inc(s["ve2_ready"], 1)

            def make_yhat(t):
                n = TILES[t][2]
                dve.wait_ge(s["rs2_ready"], t + 1)
                v.tensor_scalar(yhat[0:n, t, :], h1[0:n, t, :], mv2[0:n, t, 0:1], rs2[0:n, t:t + 1],
                                ALU.subtract, ALU.mult).then_inc(s["yhat_ready"], 1)

            def f_low(t):
                _, t0, n = TILES[t]
                dve.wait_ge(s["fhi_ready"], t + 1)
                v.tensor_tensor(f_lo[:, :, t0:t0 + n], ps_yt(t)[:, :, 0:n], f_hi[:, :, t0:t0 + n].bitcast(F32),
                                ALU.subtract).then_inc(s["flo_ready"], 1)

            def square_of(i):
                g = i // MF
                dve.wait_ge(s["relu_ready"], i + 1)
                if i >= NBUF and (i - NBUF) % 3 != 2:
                    dve.wait_ge(s["hidlo_pool"], by_pool(i - NBUF + 1))
                elif i >= NBUF:
                    dve.wait_ge(s["hidlo_dve"], (i - NBUF + 1) // 3)
                v.tensor_tensor(square[:, i % NBUF, 0:G_TOKENS[g]], relu[:, i % NBUF, 0:G_TOKENS[g]],
                                relu[:, i % NBUF, 0:G_TOKENS[g]], ALU.mult).then_inc(s["square_ready"], 1)

            def hid_low(i):
                g, m = divmod(i, MF)
                dve.wait_ge(s["square_ready"], i + 1)
                dve.wait_ge(s["hidhi_ready"], i + 1)
                v.tensor_tensor(hid_lo[:, m, group_span(g)], square[:, i % NBUF, 0:G_TOKENS[g]],
                                hid_hi[:, m, group_span(g)].bitcast(F32),
                                ALU.subtract).then_inc(s["hidlo_dve"], 1)

            def spikes(t):
                n = TILES[t][2]
                dve.wait_ge(s["y_ready"], t + 1)
                v.tensor_scalar(count[0:n, t, :], ps_y(t)[0:n, :], thresholds[0], None,
                                ALU.is_gt).then_inc(s["count_ready"], 1)
                for j in range(1, NUM_STEPS):
                    dve.wait_ge(s["count_ready"], NUM_STEPS * t + j)
                    v.scalar_tensor_tensor(count[0:n, t, :], ps_y(t)[0:n, :], thresholds[j],
                                           count[0:n, t, :], ALU.is_gt, ALU.add).then_inc(s["count_ready"], 1)
                dve.wait_ge(s["count_ready"], NUM_STEPS * (t + 1))
                v.scalar_tensor_tensor(result[0:n, t, :], count[0:n, t, :], 1.0 / NUM_STEPS,
                                       h1[0:n, t, :], ALU.mult, ALU.add).then_inc(s["result_ready"], 1)

            dve.wait_ge(s["v_in"], 16)
            v.tensor_scalar(neg_lam[:, :], slr_lam, -1.0, None, ALU.mult).then_inc(s["neg_ready"], 1)
            dve.wait_ge(s["a_in"], 16)
            dve.wait_ge(s["const_ready"], 9)
            for i in range(5):
                if i < 3:
                    h0_add(i)
                if 1 <= i <= 3:
                    h0_moments(i - 1)
                if i < 3:
                    h0_stats(i)
                if 1 <= i <= 3:
                    h0_var(i - 1)
                if 2 <= i:
                    neg_mean(i - 2)
            take_xt(0)
            take_xt(1)
            h0_add(3)
            take_xt(2)
            h0_stats(3)
            h0_moments(3)
            h0_add(4)
            h0_var(3)
            h0_stats(4)
            h0_moments(4)
            neg_mean(3)
            h0_var(4)
            take_k(0)
            take_xt(3)
            neg_mean(4)
            shift_scores(0)
            take_xt(4)
            dve.wait_ge(s["lam_ready"], 2 * DF + 1)
            dve.wait_ge(s["xt_act"], NT)
            dve.wait_ge(s["xt_dve"], NT)
            scan(0, 0)
            scan(0, 1)
            dve.wait_ge(s["neg_ready"], 1)
            dve.wait_ge(s["pad_ready"], 2 + NG)
            make_probs(0)
            take_k(1)
            route_of()
            shift_scores(1)
            router_hidden()
            arc_shift()
            scan(1, 0)
            scan(1, 1)
            router_shift()
            arc_probs()
            router_gates()
            gated_context(0)
            gated_arc()
            make_probs(1)
            dve.wait_ge(s["b_in"], 16)
            rms_arg(0)
            rms_arg(1)
            mixer_out(0)
            rms_arg(2)
            mixer_out(1)
            mixer_add(0)
            mixer_out(2)
            mixer_add(1)
            mixer_add(2)
            take_mean(0)
            gated_context(1)
            h1_add(0)
            rms_arg(3)
            h1_stats(0)
            h1_add(1)
            h1_moments(0)
            rms_arg(4)
            h1_var(0)
            h1_stats(1)
            h1_add(2)
            h1_moments(1)
            h1_stats(2)
            h1_var(1)
            h1_moments(2)
            mixer_out(3)
            h1_var(2)
            make_yhat(0)
            make_yhat(1)
            mixer_out(4)
            make_yhat(2)
            mixer_add(3)
            f_low(0)
            mixer_add(4)
            f_low(1)
            f_low(2)
            take_mean(1)
            square_of(0)
            h1_add(3)
            h1_add(4)
            h1_stats(3)
            h1_stats(4)
            h1_moments(3)
            h1_moments(4)
            h1_var(3)
            h1_var(4)
            square_of(1)
            make_yhat(3)
            make_yhat(4)
            square_of(2)
            hid_low(2)
            for i in range(3, NG * MF):
                square_of(i)
                if i % 3 == 2:
                    hid_low(i)
                if i == 4:
                    f_low(3)
                    f_low(4)
            for t in range(NT):
                spikes(t)


def lay_out(i):
    def chunks(w):
        w = np.asarray(w)
        return w.reshape(w.shape[0] // P, P, w.shape[1]).transpose(1, 0, 2)

    def flat(w):
        return chunks(w).reshape(P, -1)

    def rows(x, n):
        return np.broadcast_to(np.asarray(x).reshape(1, n), (P, n))

    x = np.asarray(i["x"]).reshape(B, 3, GRID, PATCH, GRID, PATCH)
    x = x.transpose(1, 3, 5, 0, 2, 4).reshape(KP * P, T)
    cols = [np.asarray(i[n]).reshape(DF, P).T for n in ("L0_tok_b1", "L0_attn_w_norm_in")]
    lam = np.repeat(np.asarray(i["L0_attn_lambdas"]), D // HEADS).reshape(DF, P).T
    qk = np.concatenate([np.asarray(i["L0_attn_slr_" + n]) for n in ("wq1", "wq2", "wk1", "wk2")], axis=1)
    lmwo = np.concatenate([np.asarray(i["L0_attn_landmarks"]), np.asarray(i["L0_attn_slr_wo"])], axis=0).T
    arrays = {
        "vectors": np.concatenate([*cols, lam, rows(i["L0_attn_router_b2"], 3),
                                   rows(i["L0_attn_slr_lam"], 1)], axis=1),
        "patches0_w1": np.concatenate([chunks(i["L0_tok_W1"]), chunks(x)[:, :, 0:G_TOKENS[0]]], axis=2).reshape(P, -1),
        "patches1": chunks(x)[:, :, G_TOKENS[0]:].reshape(P, -1),
        "pack_a": np.concatenate([flat(i["L0_tok_W2"]), rows(i["L0_tok_b2"], D)], axis=1),
        "pack_b": np.concatenate([flat(qk), flat(i["L0_attn_slr_wv"]), flat(i["L0_attn_router_w1"]), flat(lmwo),
                                  np.asarray(i["L0_attn_router_w2"]), rows(i["L0_attn_w_norm_out"], D)], axis=1),
        "pack_c": np.concatenate([flat(i["L0_attn_mix_w"]), np.asarray(i["L0_attn_bus_compress"]).T,
                                  np.asarray(i["L0_attn_bus_publish"]).T, np.asarray(i["L0_attn_bus_expand"])], axis=1),
        "w_fc": flat(np.asarray(i["L0_ffn_W_fc"]).T),
        "w_proj": flat(np.asarray(i["L0_ffn_W_proj"]).T),
    }
    return {n: np.ascontiguousarray(v) for n, v in arrays.items()}


def kernel(**inputs):
    import concourse.bacc as bacc
    from concourse.bass_utils import run_bass_kernel_spmd

    nc = bacc.Bacc("TRN2", target_bir_lowering=False, num_devices=1)
    arrays = {n + "_dram": v for n, v in lay_out(inputs).items()}
    args = [nc.dram_tensor(n, v.shape, mybir.dt.from_np(v.dtype), kind="ExternalInput").ap()
            for n, v in arrays.items()]
    out = nc.dram_tensor("out_dram", (T, D), F32, kind="ExternalOutput").ap()
    build(nc, *args, out)
    r = run_bass_kernel_spmd(nc, [arrays], core_ids=[0])
    return r.results[0]["out_dram"].reshape(B, S, D)
```

```python
from contextlib import ExitStack

import numpy as np

import concourse.bass as bass
from concourse import mybir

ALU = mybir.AluOpType
ACT = mybir.ActivationFunctionType
F32 = mybir.dt.float32
F32R = mybir.dt.float32r
AX = mybir.AxisListType

P = 128
D = 256
DF = D // P
B = 16
GRID = 6
S = GRID * GRID
T = B * S
PATCH = 16
KP = 3 * PATCH * PATCH // P
DH = 32
SLOTS = 64
BUS = 128
F = 1024
MF = F // P
PAIR = 2 * S
NPAIR = B // 2
HALF = 64
HEADS = 8
EPS_LN = 1e-5
EPS_RMS = 1.1920929e-07
BETA, THRESHOLD, NUM_STEPS = 0.9, 1.0, 5

G_IMAGES = (10, 6)
G_TILES = (3, 2)
G_FIRST = (0, G_IMAGES[0])
G_TOKENS = tuple(n * S for n in G_IMAGES)
G_AT = (0, G_TOKENS[0])
NG = len(G_IMAGES)
NB = max(G_IMAGES)
NT = sum(G_TILES)
GT = max(G_TOKENS)
TILES = [(g, G_AT[g] + j * (G_TOKENS[g] // G_TILES[g]), G_TOKENS[g] // G_TILES[g])
         for g in range(NG) for j in range(G_TILES[g])]
TILES_OF = [[t for t, tile in enumerate(TILES) if tile[0] == g] for g in range(NG)]
PAIRS_OF = [range(G_FIRST[g] // 2, (G_FIRST[g] + G_IMAGES[g]) // 2) for g in range(NG)]
NBUF = 3
WARM = 8
WC = 512

W2_AT, B2_AT = 0, DF * D
PACK_A = B2_AT + D
VEC = 3 * DF + 3 + 1
QK_AT = 0
V_AT = QK_AT + DF * P
R1_AT = V_AT + DF * DH
LW_AT = R1_AT + DF * P
R2_AT = LW_AT + DF * (SLOTS + DH)
WO_AT = R2_AT + 3
PACK_B = WO_AT + D
BUS_AT = 2 * DF * D
PACK_C = BUS_AT + D + BUS + D


def group_span(g):
    return slice(G_AT[g], G_AT[g] + G_TOKENS[g])


def spike_thresholds():
    f = np.float32

    def count(y):
        mem, spikes = f(0), 0
        for _ in range(NUM_STEPS):
            reset = f(mem - f(THRESHOLD) > 0)
            mem = f(f(f(BETA) * mem) + y) - reset * f(THRESHOLD)
            spikes += int(mem - f(THRESHOLD) > 0)
        return spikes

    steps = []
    for n in range(1, NUM_STEPS + 1):
        low, high = f(0), f(2 * THRESHOLD)
        while np.nextafter(low, high) < high:
            mid = f((low + high) / 2)
            if count(mid) >= n:
                high = mid
            else:
                low = mid
        steps.append(float(low))
    return steps


def build(nc, v_d, pw0_d, pw1_d, a_d, b_d, c_d, f_d, p_d, out_d):
    thresholds = spike_thresholds()
    ctx = ExitStack()
    with ctx:
        def sb(name, shape, dtype=F32):
            return ctx.enter_context(nc.sbuf_tensor(name, shape, dtype))

        def sem(name):
            return ctx.enter_context(nc.semaphore(name))

        W0 = D + G_TOKENS[0]
        PW = KP * (D + T)
        pw = sb("patches_and_w1", [P, PW])
        pw_hi = sb("pw_hi", [P, PW], F32R)
        pw_lo = sb("pw_lo", [P, PW], F32R)

        def w1_of(x, k, m):
            return x[:, k * W0 + m * P:k * W0 + (m + 1) * P]

        def patches_of(x, k, g):
            at = k * W0 + D if g == 0 else KP * W0 + k * G_TOKENS[1]
            return x[:, at:at + G_TOKENS[g]]

        hid_hi = pw_hi[:, 0:MF * T].rearrange("p (m n) -> p m n", m=MF)
        hid_lo = pw_lo[:, 0:MF * T].rearrange("p (m n) -> p m n", m=MF)

        vec = sb("vectors", [P, VEC])
        wa = sb("pack_a", [P, PACK_A])
        wb = sb("pack_b", [P, PACK_B])
        wc = sb("pack_c", [P, PACK_C])
        wf = pw[:, 0:DF * F]
        wp = pw[:, DF * F:DF * F + MF * D]
        wf_hi, wf_lo = sb("wf_hi", [P, DF * F], F32R), sb("wf_lo", [P, DF * F], F32R)
        wp_hi, wp_lo = sb("wp_hi", [P, MF * D], F32R), sb("wp_lo", [P, MF * D], F32R)
        w2 = wa[:, W2_AT:B2_AT].rearrange("p (k n) -> p k n", k=DF)
        b2 = wa[:, B2_AT:PACK_A]
        b1, w_in, lam = vec[:, 0:2], vec[:, 2:4], vec[:, 4:6]
        rb2, slr_lam = vec[:, 6:9], vec[:, 9:10]
        wqk = wb[:, QK_AT:V_AT].rearrange("p (k n) -> p k n", k=DF)
        wv = wb[:, V_AT:R1_AT].rearrange("p (k n) -> p k n", k=DF)
        rw1 = wb[:, R1_AT:LW_AT].rearrange("p (k n) -> p k n", k=DF)
        lmwo = wb[:, LW_AT:R2_AT].rearrange("p (k n) -> p k n", k=DF)
        rw2 = wb[:, R2_AT:WO_AT]
        w_out = wb[:, WO_AT:PACK_B]
        mix = wc[:, 0:BUS_AT].rearrange("p (k n) -> p k n", k=2 * DF)
        compress_t = wc[:, BUS_AT:BUS_AT + D]
        publish_t = wc[:, BUS_AT + D:BUS_AT + D + BUS]
        expand = wc[:, BUS_AT + D + BUS:PACK_C]

        ident = sb("ident", [P, P])
        image_sum = sb("image_sum", [P, NT, B])
        image_row = sb("image_row", [NB, GT])
        minus_half = sb("minus_half", [P, 2])
        warm = sb("warm", [P, 512], mybir.dt.bfloat16)
        loaded = sb("loaded", [P, 2])
        var_scale = sb("var_scale", [P, 2])
        var_shift = sb("var_shift", [P, 2])
        lam_scan = sb("lam_scan", [P, DF, GT])
        one_minus_lam = sb("one_minus_lam", [P, DF])
        mix_ssm = sb("mix_ssm", [P, DF, D])
        rw2_b = sb("rw2_b", [P, 3, P])
        neg_lam = sb("neg_lam", [P, 1])

        hidden = sb("hidden", [P, DF, T])
        h0 = sb("h0", [P, NT, D])
        stats = sb("stats", [P, NT, 6])
        mv = sb("mv", [P, NT, 2])
        ve = sb("ve", [P, NT, 2])
        rs = sb("rs", [P, NT, 2])
        nm = sb("nm", [P, NT, 2])
        xhat = sb("xhat", [P, NT, D])
        xT = sb("xT", [P, DF, T])
        a = sb("a", [P, NT, D])
        out2 = sb("out2", [P, NT, D])
        lmwo_mix = sb("lmwo_mix", [SLOTS + DH, D])
        pub_exp = sb("pub_exp", [BUS, D])
        bus_w = sb("bus_w", [P, DF, D])
        Q_AT = [G_AT[g] + g * (HALF - S) for g in range(NG)]
        qs = sb("qs", [2 * DH, T + NG * (HALF - S)])
        ks = sb("ks", [2 * DH, T])
        vs = sb("vs", [PAIR, NPAIR, DH])
        route = sb("route", [P, DF, B])
        rhid, rexp, rden, rrec = (sb(n, [P, B]) for n in ("rhid", "rexp", "rden", "rrec"))
        lg = sb("lg", [P, B, 3])
        lgm = sb("lgm", [P, B])
        lgd = sb("lgd", [P, B, 3])
        lge = sb("lge", [P, B, 3])
        lgs = sb("lgs", [P, B])
        lgr = sb("lgr", [P, B])
        gate = sb("gate", [P, B])
        gsum = sb("gsum", [P, B])
        p_full = sb("p_full", [P, B])
        smax = sb("smax", [P, 2, NPAIR])
        sh = sb("sh", [P, 2, NPAIR, S])
        se = sb("se", [P, 2, NPAIR, S])
        ssum = sb("ssum", [P, 2, NPAIR])
        srec = sb("srec", [P, 2, NPAIR])
        sfac = sb("sfac", [P, NPAIR])
        sp = sb("sp", [P, 2, NPAIR, S])
        probs = sb("probs", [P, NPAIR, PAIR])
        probs_t = sb("probs_t", [PAIR, NPAIR, PAIR])
        arc_m = sb("arc_m", [NB, NG])
        arc_b = sb("arc_b", [NB, NG])
        arc_e = sb("arc_e", [NB, NG, SLOTS])
        arc_s = sb("arc_s", [NB, NG])
        arc_r = sb("arc_r", [NB, NG])
        arc_p = sb("arc_p", [NB, NG, SLOTS])
        comb = sb("comb", [SLOTS + DH, T])
        ssm = sb("ssm", [P, DF, T])
        sqj = sb("sqj", [P, D])
        ssq = sb("ssq", [P, NT])
        rve = sb("rve", [P, NT])
        rr = sb("rr", [P, NT])
        rms = sb("rms", [P, NT, D])
        h1p = sb("h1p", [P, NT, D])
        mean = sb("mean", [P, NG, DF, NB])
        row = sb("row", [NB, NG, D])
        h1 = h1p
        stats2 = sb("stats2", [P, NT, 6])
        mv2 = sb("mv2", [P, NT, 2])
        ve2 = sb("ve2", [P, NT])
        rs2 = sb("rs2", [P, NT])
        yhat = rms
        f_hi, f_lo = sb("f_hi", [P, DF, T], F32R), sb("f_lo", [P, DF, T], F32R)
        relu = sb("relu", [P, NBUF, GT])
        square = sb("square", [P, NBUF, GT])
        count, result = xhat, a

        bank = [ctx.enter_context(nc.psum_tensor(f"bank{i}", [P, 512], F32)) for i in range(8)]

        def ps_z(g, m):
            return bank[2 * g + m][:, 0:G_TOKENS[g]]

        XT_BANKS = [6, 0, 4, 0, 0]
        H_BANKS = [4, 5, 4, 2, 3]

        def ps_h(t):
            return bank[H_BANKS[t]][:, 0:D]

        def ps_xt(t, f):
            if t in TILES_OF[0]:
                return bank[XT_BANKS[t] + f][:, 0:P]
            return bank[XT_BANKS[t]][:, f * P:(f + 1) * P]

        ps_qk = [bank[0][:, 0:n] for n in G_TOKENS]
        ps_v = [bank[1][0:PAIR, 0:len(js) * DH] for js in PAIRS_OF]
        ps_lw = bank[7][0:SLOTS + DH, D:2 * D]
        ps_pe = bank[6][:, D:2 * D]
        ps_bus = bank[1][:, :].rearrange("p (f n) -> p f n", f=DF)

        def ps_s(g, i):
            n = len(PAIRS_OF[g])
            return bank[6 + i][:, 0:n * S].rearrange("p (j k) -> p j k", j=n)

        def images_of(g):
            return slice(G_FIRST[g], G_FIRST[g] + G_IMAGES[g])

        def ps_hid(g):
            return bank[5][:, 0:B][:, images_of(g)]

        def ps_lg(g):
            return bank[5][:, B:4 * B].rearrange("p (j b) -> p j b", j=3)[:, :, images_of(g)]

        def ps_arc(g):
            return bank[4][0:G_IMAGES[g], 0:SLOTS]

        def ps_arct(g):
            return bank[4][0:SLOTS, SLOTS:SLOTS + G_IMAGES[g]]

        PT = [[(0, PAIRS_OF[0][0:3]), (1, PAIRS_OF[0][3:])], [(1, PAIRS_OF[1])]]

        def ps_pt(b, n):
            return bank[b][0:PAIR, 0:n * P].rearrange("p (j q) -> p j q", j=n)

        def ps_c(g):
            return bank[(7, 5)[g]][SLOTS:SLOTS + DH, 0:G_TOKENS[g]]

        O_AT = [(2, 0), (2, D), (3, 0), (6, 0), (6, D)]
        Y_PARTS = [(0, 0, D, 4), (1, 0, D, 5), (2, 0, D, 6), (3, 0, D, 7), (4, 0, D, 4)]
        X_BANKS = [2, 0, 3, 6, 7]
        YT_BANKS = [7, 4, 5, 1, 0]
        FC_BANKS = [0, 2, 3]

        def ps_o(t):
            b_, at = O_AT[t]
            return bank[b_][:, at:at + D]

        def ps_x(t):
            return bank[X_BANKS[t]][:, 0:D]

        def ps_m(g, f):
            return bank[5][:, f * NB:f * NB + G_IMAGES[g]]

        def ps_row(g):
            return bank[5][0:G_IMAGES[g], D:2 * D]

        def ps_yt(t):
            return bank[YT_BANKS[t]][:, 0:D].rearrange("p (f n) -> p f n", f=DF)

        def ps_f(i):
            return bank[FC_BANKS[i % len(FC_BANKS)]][:, 0:G_TOKENS[i // MF]]

        def ps_y(i):
            t, _, cols, b_ = Y_PARTS[i]
            return bank[b_][0:TILES[t][2], 0:cols]

        names = """v_in warm_ready out2_ready row_ready row_taken a_in b_in c_in f_in p_in const_zero
        const_ready pad_ready lam_ready mixs_ready rw2b_ready w1lo_ready pwhi_ready pwlo_ready
        wfhi_ready wflo_ready wphi_ready wplo_ready z_ready hidden_ready h_ready h0_ready
        stats_ready mv_ready ve_ready rs_ready nm_ready xhat_ready a_ready xt_ready xt_act xt_dve
        lw_ready pe_ready bus_ready lw_taken pe_taken bus_taken qk_ready q_taken k_taken v_ready
        v_taken route_ready r_ready rexp_ready rden_ready rrec_ready rhid_ready lg_ready lg_added
        lg_max lg_shift lg_exp lg_sum lg_gsum lg_rec gate_ready pfull_ready s_ready smax_ready
        sh_ready se_ready ssum_ready srec_ready sfac_ready neg_ready sp_ready probs_ready pt_ready
        pt_taken c_ready c_taken arc_ready arcm_ready arcb_ready arce_ready arcr_ready arcp_ready
        arct_ready arc_taken ssm_ready o_ready ssq_ready rve_ready rr_ready rms_ready h1p_ready
        m_ready mean_ready x_ready h1_ready stats2_ready mv2_ready ve2_ready rs2_ready yhat_ready
        yt_ready fhi_ready flo_ready fc_ready relu_ready square_ready hidhi_ready hidlo_pool
        hidlo_dve y_ready count_ready result_ready out_sem""".split()
        s = {n: sem(n) for n in names}
        pw0_in = [sem(f"pw0_in{k}") for k in range(KP)]
        pw1_in = [sem(f"pw1_in{h}") for h in range(2)]
        K1 = KP // 2
        G1 = KP * W0

        def by_pool(n):
            return n - n // 3

        block = ctx.enter_context(nc.Block())

        @block.sync
        def _(sp_):
            for k in range(KP):
                sp_.dma_start(pw[:, k * W0:(k + 1) * W0], pw0_d[:, k * W0:(k + 1) * W0]).then_inc(pw0_in[k], 16)
            n = K1 * G_TOKENS[1]
            for h in range(2):
                sp_.dma_start(pw[:, G1 + h * n:G1 + (h + 1) * n], pw1_d[:, h * n:(h + 1) * n]).then_inc(pw1_in[h], 16)
                if h == 0:
                    sp_.dma_start(wa[:, :], a_d).then_inc(s["a_in"], 16)
            sp_.dma_start(wb[:, :], b_d).then_inc(s["b_in"], 16)
            sp_.dma_start(wc[:, :], c_d).then_inc(s["c_in"], 16)
            sp_.wait_ge(s["w1lo_ready"], KP)
            sp_.wait_ge(s["pwlo_ready"], KP + 2)
            sp_.dma_start(wf[:, :], f_d).then_inc(s["f_in"], 16)
            sp_.dma_start(wp[:, :], p_d).then_inc(s["p_in"], 16)
            for i, (t, c0, cols, _) in enumerate(Y_PARTS):
                _, t0, n = TILES[t]
                sp_.wait_ge(s["result_ready"], i + 1)
                sp_.dma_start(out_d[t0:t0 + n, c0:c0 + cols], result[0:n, t, c0:c0 + cols]).then_inc(s["out_sem"], 16)
            sp_.wait_ge(s["out_sem"], 16 * len(Y_PARTS))

        @block.gpsimd
        def _(pool):
            g_ = nc.gpsimd
            g_.memset(warm[:, :], 0.5).then_inc(s["warm_ready"], 1)
            g_.memset(loaded[:, :], 0.0).then_inc(s["warm_ready"], 1)
            for k in range(KP):
                pool.wait_ge(s["pwhi_ready"], k + 1)
                g_.tensor_tensor(pw_lo[:, k * W0:k * W0 + D], pw[:, k * W0:k * W0 + D],
                                 pw_hi[:, k * W0:k * W0 + D].bitcast(F32), ALU.subtract).then_inc(s["w1lo_ready"], 1)
            g_.memset(ident[:, :], 0.0).then_inc(s["const_zero"], 1)
            g_.memset(image_sum[:, :, :], 1.0).then_inc(s["const_zero"], 1)
            g_.memset(image_row[:, :], 1.0).then_inc(s["const_zero"], 1)
            g_.memset(minus_half[:, :], -0.5).then_inc(s["const_ready"], 1)
            g_.memset(var_scale[:, 0:1], 1.0).then_inc(s["const_ready"], 1)
            g_.memset(var_scale[:, 1:2], 1.0 + EPS_RMS).then_inc(s["const_ready"], 1)
            g_.memset(var_shift[:, 0:1], EPS_LN).then_inc(s["const_ready"], 1)
            g_.memset(var_shift[:, 1:2], EPS_RMS * EPS_LN).then_inc(s["const_ready"], 1)
            pool.wait_ge(s["const_zero"], 3)
            g_.affine_select(out=ident[:, :], in_=ident[:, :], compare_op=ALU.not_equal, fill=1.0,
                             base=0, pattern=[[-1, P]], channel_multiplier=1).then_inc(s["const_ready"], 1)
            for g in range(NG):
                t_, n_ = TILES_OF[g][0], TILES[TILES_OF[g][0]][2]
                part = image_sum[:, t_:t_ + G_TILES[g], :]
                g_.affine_select(out=part, in_=part, compare_op=ALU.is_ge, fill=0.0, base=G_AT[g],
                                 pattern=[[n_, G_TILES[g]], [-S, B]],
                                 channel_multiplier=1).then_inc(s["const_zero"], 1)
            g_.affine_select(out=image_row[:, :], in_=image_row[:, :], compare_op=ALU.is_ge, fill=0.0,
                             base=0, pattern=[[1, GT]], channel_multiplier=-S).then_inc(s["const_zero"], 1)
            pool.wait_ge(s["const_zero"], 6)
            for g in range(NG):
                t_, n_ = TILES_OF[g][0], TILES[TILES_OF[g][0]][2]
                part = image_sum[:, t_:t_ + G_TILES[g], :]
                g_.affine_select(out=part, in_=part, compare_op=ALU.is_ge, fill=0.0, base=S - 1 - G_AT[g],
                                 pattern=[[-n_, G_TILES[g]], [S, B]],
                                 channel_multiplier=-1).then_inc(s["const_ready"], 1)
            g_.affine_select(out=image_row[:, :], in_=image_row[:, :], compare_op=ALU.is_ge, fill=0.0,
                             base=S - 1, pattern=[[-1, GT]], channel_multiplier=S).then_inc(s["const_ready"], 1)
            pool.wait_ge(s["v_in"], 16)
            for f in range(DF):
                g_.tensor_copy(lam_scan[:, f, :], lam[:, f:f + 1].to_broadcast([P, GT])).then_inc(s["lam_ready"], 1)

            def ln_power(t):
                n = TILES[t][2]
                pool.wait_ge(s["ve_ready"], t + 1)
                g_.tensor_tensor(rs[0:n, t, :], ve[0:n, t, :], minus_half[0:n, :], ALU.pow).then_inc(s["rs_ready"], 1)

            def rms_power(t):
                n = TILES[t][2]
                pool.wait_ge(s["rve_ready"], t + 1)
                g_.tensor_tensor(rr[0:n, t:t + 1], rve[0:n, t:t + 1], minus_half[0:n, 0:1],
                                 ALU.pow).then_inc(s["rr_ready"], 1)

            def add_residual(t):
                n = TILES[t][2]
                pool.wait_ge(s["out2_ready"], t + 1)
                g_.tensor_tensor(h1p[0:n, t, :], out2[0:n, t, :], h0[0:n, t, :], ALU.add).then_inc(s["h1p_ready"], 1)

            def ln2_power(t):
                n = TILES[t][2]
                pool.wait_ge(s["ve2_ready"], t + 1)
                g_.tensor_tensor(rs2[0:n, t:t + 1], ve2[0:n, t:t + 1], minus_half[0:n, 0:1],
                                 ALU.pow).then_inc(s["rs2_ready"], 1)

            def low_part(w, hi, lo, c, hi_ready, lo_ready):
                pool.wait_ge(hi_ready, c + 1)
                at = slice(c * WC, (c + 1) * WC)
                g_.tensor_tensor(lo[:, at], w[:, at], hi[:, at].bitcast(F32), ALU.subtract).then_inc(lo_ready, 1)

            def wf_low(c):
                low_part(wf, wf_hi, wf_lo, c, s["wfhi_ready"], s["wflo_ready"])

            def wp_low(c):
                low_part(wp, wp_hi, wp_lo, c, s["wphi_ready"], s["wplo_ready"])

            def hid_low(i):
                g, m = divmod(i, MF)
                pool.wait_ge(s["square_ready"], i + 1)
                pool.wait_ge(s["hidhi_ready"], i + 1)
                g_.tensor_tensor(hid_lo[:, m, group_span(g)], square[:, i % NBUF, 0:G_TOKENS[g]],
                                 hid_hi[:, m, group_span(g)].bitcast(F32),
                                 ALU.subtract).then_inc(s["hidlo_pool"], 1)

            for t in TILES_OF[0]:
                ln_power(t)
            pool.wait_ge(s["lam_ready"], DF)
            for f in range(DF):
                g_.memset(lam_scan[:, f, :].rearrange("p (b s) -> p b s", s=S)[:, :, 0:1],
                          0.0).then_inc(s["lam_ready"], 1)
            g_.tensor_scalar(one_minus_lam[:, :], lam, -1.0, 1.0, ALU.mult, ALU.add).then_inc(s["lam_ready"], 1)
            g_.memset(probs[:, :, :], 0.0).then_inc(s["pad_ready"], 1)
            g_.memset(comb[0:SLOTS, :], 0.0).then_inc(s["pad_ready"], 1)
            for g in range(NG):
                at = Q_AT[g] + G_TOKENS[g]
                g_.memset(qs[:, at:at + HALF - S], 0.0).then_inc(s["pad_ready"], 1)
            pool.wait_ge(s["b_in"], 16)
            for j in range(3):
                g_.tensor_copy(rw2_b[:, j, :], rw2[:, j:j + 1].to_broadcast([P, P])).then_inc(s["rw2b_ready"], 1)
            pool.wait_ge(s["c_in"], 16)
            pool.wait_ge(s["lam_ready"], 2 * DF + 1)
            for f in range(DF):
                g_.tensor_scalar(mix_ssm[:, f, :], mix[:, f, :], one_minus_lam[:, f:f + 1], None,
                                 ALU.mult).then_inc(s["mixs_ready"], 1)
            for t in TILES_OF[1]:
                ln_power(t)
            for c in range(2):
                wf_low(c)
            for t in TILES_OF[0]:
                rms_power(t)
            for t in TILES_OF[0]:
                add_residual(t)
            wf_low(2)
            wf_low(3)
            wp_low(0)
            wp_low(1)
            ln2_power(0)
            ln2_power(1)
            ln2_power(2)
            wp_low(2)
            wp_low(3)
            hid_low(0)
            rms_power(3)
            rms_power(4)
            hid_low(1)
            hid_low(3)
            hid_low(4)
            add_residual(3)
            add_residual(4)
            hid_low(6)
            hid_low(7)
            for t in TILES_OF[1]:
                ln2_power(t)
            for i in range(MF, NG * MF):
                if i % 3 != 2:
                    hid_low(i)

        @block.scalar
        def _(act):
            e = nc.scalar
            act.dma_start(vec[:, :], v_d).then_inc(s["v_in"], 16)
            act.wait_ge(s["warm_ready"], 2)
            e.activation(loaded[:, 0:1], loaded[:, 1:2], ACT.Silu)
            for k in range(KP):
                act.wait_ge(pw0_in[k], 16)
                e.activation(pw_hi[:, k * W0:(k + 1) * W0], pw[:, k * W0:(k + 1) * W0],
                             ACT.Copy).then_inc(s["pwhi_ready"], 1)

            def patches_high(h):
                n1 = K1 * G_TOKENS[1]
                at = slice(G1 + h * n1, G1 + (h + 1) * n1)
                act.wait_ge(pw1_in[h], 16)
                e.activation(pw_hi[:, at], pw[:, at], ACT.Copy).then_inc(s["pwhi_ready"], 1)

            def silu(g):
                for m in range(DF):
                    act.wait_ge(s["z_ready"], g * DF + m + 1)
                    e.activation(hidden[:, m, group_span(g)], ps_z(g, m), ACT.Silu,
                                 bias=b1[:, m:m + 1]).then_inc(s["hidden_ready"], 1)

            def normed(t):
                n = TILES[t][2]
                act.wait_ge(s["nm_ready"], t + 1)
                e.activation(xhat[0:n, t, :], h0[0:n, t, :], ACT.Identity, bias=nm[0:n, t, 1:2],
                             scale=rs[0:n, t, 1:2]).then_inc(s["xhat_ready"], 1)

            def layernorm(t):
                n = TILES[t][2]
                e.activation(a[0:n, t, :], h0[0:n, t, :], ACT.Identity, bias=nm[0:n, t, 0:1],
                             scale=rs[0:n, t, 0:1]).then_inc(s["a_ready"], 1)

            def take_xt(t):
                _, t0, n = TILES[t]
                act.wait_ge(s["xt_ready"], t + 1)
                for f in range(1 if t in TILES_OF[0] else DF):
                    last = e.activation(xT[:, f, t0:t0 + n], ps_xt(t, f)[:, 0:n], ACT.Copy,
                                        scale=w_in[:, f:f + 1])
                last.then_inc(s["xt_act"], 1)

            def take_q(g):
                act.wait_ge(s["qk_ready"], g + 1)
                e.activation(qs[:, Q_AT[g]:Q_AT[g] + G_TOKENS[g]], ps_qk[g][0:2 * DH, :], ACT.Copy,
                             scale=float(DH) ** -0.5).then_inc(s["q_taken"], 1)

            def take_v(g):
                act.wait_ge(s["v_ready"], g + 1)
                j0, n = PAIRS_OF[g][0], len(PAIRS_OF[g])
                e.activation(vs[:, j0:j0 + n, :].rearrange("p j d -> p (j d)"), ps_v[g],
                             ACT.Copy).then_inc(s["v_taken"], 1)

            def router_hidden(g):
                act.wait_ge(s["r_ready"], g + 1)
                e.activation(rexp[:, images_of(g)], ps_hid(g), ACT.Exp, scale=-1.0 / S).then_inc(s["rexp_ready"], 1)

            def exps(g):
                j0, n = PAIRS_OF[g][0], len(PAIRS_OF[g])
                act.wait_ge(s["sh_ready"], g + 1)
                e.activation(se[:, :, j0:j0 + n, :], sh[:, :, j0:j0 + n, :], ACT.Exp).then_inc(s["se_ready"], 1)

            def exp_router(g):
                act.wait_ge(s["lg_shift"], g + 1)
                e.activation(lge[:, images_of(g), :], lgd[:, images_of(g), :], ACT.Exp).then_inc(s["lg_exp"], 1)

            def exp_arc(g):
                nb = G_IMAGES[g]
                act.wait_ge(s["arcb_ready"], g + 1)
                e.activation(arc_e[0:nb, g, :], ps_arc(g), ACT.Exp, bias=arc_b[0:nb, g:g + 1],
                             scale=float(D) ** -0.5, accum_out=arc_s[0:nb, g:g + 1]).then_inc(s["arce_ready"], 1)

            def take_probs(n_, g, part):
                act.wait_ge(s["pt_ready"], n_ + 1)
                b_, js = PT[g][part]
                e.activation(probs_t[:, js[0]:js[0] + len(js), :].rearrange("k j (i q) -> k j i q", i=2),
                             ps_pt(b_, len(js)).rearrange("k j (i q) -> k j i q", i=2)[:, :, :, 0:S],
                             ACT.Copy).then_inc(s["pt_taken"], 1)

            def squares(t):
                n = TILES[t][2]
                act.wait_ge(s["o_ready"], [1, 1, 2, 3, 3][t])
                if t >= 1:
                    act.wait_ge(s["ssq_ready"], t)
                e.activation(sqj[0:n, :], ps_o(t)[0:n, :], ACT.Square, scale=float(D) ** -0.5,
                             accum_out=ssq[0:n, t:t + 1]).then_inc(s["ssq_ready"], 1)

            def take_row(g):
                nb = G_IMAGES[g]
                act.wait_ge(s["row_ready"], g + 1)
                e.activation(row[0:nb, g, :], ps_row(g), ACT.Copy).then_inc(s["row_taken"], 1)

            def take_h1(t):
                n = TILES[t][2]
                act.wait_ge(s["x_ready"], t + 1)
                e.activation(h1[0:n, t, :], ps_x(t)[0:n, :], ACT.Copy).then_inc(s["h1_ready"], 1)

            def f_high(t):
                _, t0, n = TILES[t]
                act.wait_ge(s["yt_ready"], t + 1)
                e.activation(f_hi[:, :, t0:t0 + n], ps_yt(t)[:, :, 0:n], ACT.Copy).then_inc(s["fhi_ready"], 1)

            def high_part(w, hi, c, ready):
                at = slice(c * WC, (c + 1) * WC)
                e.activation(hi[:, at], w[:, at], ACT.Copy).then_inc(ready, 1)

            def relu_of(i):
                g = i // MF
                act.wait_ge(s["fc_ready"], i + 1)
                if i >= NBUF:
                    act.wait_ge(s["square_ready"], i - NBUF + 1)
                e.activation(relu[:, i % NBUF, 0:G_TOKENS[g]], ps_f(i), ACT.Relu).then_inc(s["relu_ready"], 1)

            def hid_high(i):
                g, m = divmod(i, MF)
                act.wait_ge(s["relu_ready"], i + 1)
                e.activation(hid_hi[:, m, group_span(g)], relu[:, i % NBUF, 0:G_TOKENS[g]],
                             ACT.Square).then_inc(s["hidhi_ready"], 1)

            act.wait_ge(s["v_in"], 16)
            patches_high(0)
            silu(0)
            patches_high(1)
            for t in TILES_OF[0]:
                normed(t)
            for t in TILES_OF[0]:
                take_xt(t)
            silu(1)
            act.wait_ge(s["lw_ready"], 1)
            act.wait_ge(s["xt_dve"], 1)
            e.activation(lmwo_mix[:, :], ps_lw, ACT.Copy).then_inc(s["lw_taken"], 1)
            act.wait_ge(s["pe_ready"], 1)
            e.activation(pub_exp[:, :], ps_pe, ACT.Copy).then_inc(s["pe_taken"], 1)
            take_q(0)
            e.activation(loaded[:, 0:1], loaded[:, 1:2], ACT.Exp)
            router_hidden(0)
            exps(0)
            normed(3)
            take_v(0)
            take_xt(3)
            normed(4)
            take_xt(4)
            exp_router(0)
            exp_arc(0)
            take_probs(0, 0, 0)
            take_probs(1, 0, 1)
            act.wait_ge(s["f_in"], 16)
            high_part(wf, wf_hi, 0, s["wfhi_ready"])
            layernorm(0)
            high_part(wf, wf_hi, 1, s["wfhi_ready"])
            router_hidden(1)
            layernorm(1)
            layernorm(2)
            squares(0)
            squares(1)
            squares(2)
            take_q(1)
            act.wait_ge(s["bus_ready"], 1)
            e.activation(bus_w[:, :, :], ps_bus, ACT.Copy).then_inc(s["bus_taken"], 1)
            exp_router(1)
            exp_arc(1)
            high_part(wf, wf_hi, 2, s["wfhi_ready"])
            exps(1)
            high_part(wf, wf_hi, 3, s["wfhi_ready"])
            act.wait_ge(s["p_in"], 16)
            high_part(wp, wp_hi, 0, s["wphi_ready"])
            take_row(0)
            high_part(wp, wp_hi, 1, s["wphi_ready"])
            layernorm(3)
            high_part(wp, wp_hi, 2, s["wphi_ready"])
            for t in TILES_OF[0]:
                take_h1(t)
            take_v(1)
            high_part(wp, wp_hi, 3, s["wphi_ready"])
            layernorm(4)
            f_high(0)
            f_high(1)
            f_high(2)
            take_probs(2, 1, 0)
            for i in range(MF):
                relu_of(i)
                hid_high(i)
                if i == 1:
                    squares(3)
                    squares(4)
            take_row(1)
            f_high(3)
            f_high(4)
            for i in range(MF, NG * MF):
                relu_of(i)
                hid_high(i)

        @block.tensor
        def _(pe):
            mm = nc.tensor.matmul

            def mm_split(out, left, right, start, stop):
                mm(out, left[0], right[1], start=start, stop=False)
                mm(out, left[1], right[0], start=False, stop=False)
                return mm(out, left[0], right[0], start=False, stop=stop)

            def keep_warm(b_, n):
                for _ in range(n):
                    mm(bank[b_][:, :], warm[:, 0:P], warm[:, :], start=True, stop=True)

            def tokenizer_up(g, ks):
                for k in ks:
                    left = [(w1_of(pw_hi, k, m), w1_of(pw_lo, k, m)) for m in range(DF)]
                    right = (patches_of(pw_hi, k, g), patches_of(pw_lo, k, g))
                    if g == 0:
                        pe.wait_ge(s["pwhi_ready"], k + 1)
                    elif k % K1 == 0:
                        pe.wait_ge(s["pwhi_ready"], KP + k // K1 + 1)
                    for m in range(DF):
                        mm(ps_z(g, m), left[m][0], right[0], start=(k == 0), stop=False)
                    if g == 0:
                        pe.wait_ge(s["w1lo_ready"], k + 1)
                        pe.wait_ge(s["pwlo_ready"], k + 1)
                    elif k % K1 == 0:
                        pe.wait_ge(s["pwlo_ready"], KP + k // K1 + 1)
                    for m in range(DF):
                        mm(ps_z(g, m), left[m][0], right[1], start=False, stop=False)
                        last = mm(ps_z(g, m), left[m][1], right[0], start=False, stop=(k == KP - 1))
                        if k == KP - 1:
                            last.then_inc(s["z_ready"], 1)

            def tokenizer_down(t):
                g, t0, n = TILES[t]
                pe.wait_ge(s["hidden_ready"], DF * (g + 1))
                if t == 2:
                    pe.wait_ge(s["h0_ready"], 1)
                for k in range(DF):
                    last = mm(ps_h(t)[0:n, :], hidden[:, k, t0:t0 + n], w2[:, k, :],
                              start=(k == 0), stop=(k == DF - 1))
                last.then_inc(s["h_ready"], 1)

            def transposes(out, in_, n):
                for f in range(DF):
                    last = nc.tensor.transpose(out(f)[:, 0:n], in_[0:n, f * P:(f + 1) * P], ident[0:n, 0:n])
                return last

            def transpose_x(t):
                n = TILES[t][2]
                pe.wait_ge(s["xhat_ready"], t + 1)
                if t == 4:
                    pe.wait_ge(s["xt_act"], 4)
                transposes(lambda f: ps_xt(t, f), xhat[:, t, :], n).then_inc(s["xt_ready"], 1)

            def queries_keys(g):
                pe.wait_ge(s["xt_act"], TILES_OF[g][-1] + 1)
                pe.wait_ge(s["xt_dve"], G_TILES[0])
                if g >= 1:
                    pe.wait_ge(s["pt_taken"], 1)
                for k in range(DF):
                    last = mm(ps_qk[g], wqk[:, k, :], xT[:, k, group_span(g)],
                              start=(k == 0), stop=(k == DF - 1))
                last.then_inc(s["qk_ready"], 1)

            def values(g):
                if g >= 1:
                    pe.wait_ge(s["bus_taken"], 1)
                for jj, j in enumerate(PAIRS_OF[g]):
                    for k in range(DF):
                        last = mm(ps_v[g][:, jj * DH:(jj + 1) * DH], xT[:, k, j * PAIR:(j + 1) * PAIR],
                                  wv[:, k, :], start=(k == 0), stop=(k == DF - 1))
                last.then_inc(s["v_ready"], 1)

            def scores(g):
                pe.wait_ge(s["q_taken"], g + 1)
                pe.wait_ge(s["k_taken"], g + 1)
                if g >= 1:
                    pe.wait_ge(s["sh_ready"], g)
                    pe.wait_ge(s["c_taken"], g)
                q0 = Q_AT[g] - G_AT[g]
                for i in range(2):
                    for b in range(G_FIRST[g], G_FIRST[g] + G_IMAGES[g]):
                        row = HALF * (b % 2)
                        last = mm(ps_s(g, i)[row:row + HALF, (b - G_FIRST[g]) // 2, :],
                                  qs[i * DH:(i + 1) * DH, q0 + b * S:q0 + b * S + HALF],
                                  ks[i * DH:(i + 1) * DH, b * S:(b + 1) * S], start=True, stop=True)
                    last.then_inc(s["s_ready"], 1)

            def router_up(g):
                pe.wait_ge(s["route_ready"], g + 1)
                for k in range(DF):
                    last = mm(ps_hid(g), rw1[:, k, :], route[:, k, images_of(g)],
                              start=(k == 0), stop=(k == DF - 1))
                last.then_inc(s["r_ready"], 1)

            def router_logits(g):
                pe.wait_ge(s["rhid_ready"], g + 1)
                pe.wait_ge(s["rw2b_ready"], 3)
                for j in range(3):
                    last = mm(ps_lg(g)[:, j, :], rw2_b[:, j, :], rhid[:, images_of(g)], start=True, stop=True)
                last.then_inc(s["lg_ready"], 1)

            def arc_logits(g):
                if g >= 1:
                    pe.wait_ge(s["arc_taken"], g)
                for k in range(DF):
                    last = mm(ps_arc(g), xT[:, k, G_AT[g] + S - 1:G_AT[g] + G_TOKENS[g]:S], lmwo[:, k, 0:SLOTS],
                              start=(k == 0), stop=(k == DF - 1))
                last.then_inc(s["arc_ready"], 1)

            def arc_transpose(g):
                nb = G_IMAGES[g]
                pe.wait_ge(s["arcp_ready"], g + 1)
                nc.tensor.transpose(ps_arct(g), arc_p[0:nb, g, :], ident[0:nb, 0:nb]).then_inc(s["arct_ready"], 1)

            def transpose_probs(g):
                pe.wait_ge(s["probs_ready"], 2 * (g + 1))
                pe.wait_ge(s["v_taken"], g + 1)
                for b_, js in PT[g]:
                    for jj, j in enumerate(js):
                        last = nc.tensor.transpose(ps_pt(b_, len(js))[:, jj, :], probs[:, j, :], ident[:, :])
                    last.then_inc(s["pt_ready"], 1)

            def context(g):
                pe.wait_ge(s["v_taken"], g + 1)
                if g >= 1:
                    pe.wait_ge(s["flo_ready"], 3)
                pe.wait_ge(s["pt_taken"], len(PT[0]) if g == 0 else len(PT[0]) + len(PT[1]))
                for jj, j in enumerate(PAIRS_OF[g]):
                    last = mm(ps_c(g)[:, jj * PAIR:(jj + 1) * PAIR], vs[:, j, :], probs_t[:, j, :],
                              start=True, stop=True)
                last.then_inc(s["c_ready"], 1)

            def mixer(g, part, tiles=None):
                if part == 1:
                    pe.wait_ge(s["mixs_ready"], DF)
                    pe.wait_ge(s["ssm_ready"], DF * (g + 1))
                for t in tiles or TILES_OF[g]:
                    _, t0, n = TILES[t]
                    for k in range(DF):
                        left, right = (xT, mix[:, DF + k, :]) if part == 0 else (ssm, mix_ssm[:, k, :])
                        mm(ps_o(t)[0:n, :], left[:, k, t0:t0 + n], right,
                           start=(part == 0 and k == 0 and O_AT[t][1] == 0), stop=False,
                           skip_group_check=True)

            def mixer_end(g):
                pe.wait_ge(s["c_taken"], g + 1)
                pe.wait_ge(s["arc_taken"], g + 1)
                for t in TILES_OF[g]:
                    _, t0, n = TILES[t]
                    last = mm(ps_o(t)[0:n, :], comb[:, t0:t0 + n], lmwo_mix[:, :],
                              start=False, stop=True, skip_group_check=True)
                    if t + 1 == NT or O_AT[t + 1][0] != O_AT[t][0]:
                        last.then_inc(s["o_ready"], 1)

            def image_means(g, tiles=None):
                for t in tiles or TILES_OF[g]:
                    pe.wait_ge(s["out2_ready"], t + 1)
                    for f in range(DF):
                        n = TILES[t][2]
                        last = mm(ps_m(g, f), out2[0:n, t, f * P:(f + 1) * P],
                                  image_sum[0:n, t, G_FIRST[g]:G_FIRST[g] + G_IMAGES[g]],
                                  start=(t == TILES_OF[g][0] and f == 0), stop=(t == TILES_OF[g][-1]),
                                  skip_group_check=True)
                if t == TILES_OF[g][-1]:
                    last.then_inc(s["m_ready"], 1)

            def bus_rows(g):
                pe.wait_ge(s["mean_ready"], g + 1)
                pe.wait_ge(s["bus_taken"], 1)
                for k in range(DF):
                    last = mm(ps_row(g), mean[:, g, k, 0:G_IMAGES[g]], bus_w[:, k, :],
                              start=(k == 0), stop=(k == DF - 1))
                last.then_inc(s["row_ready"], 1)

            def residual(t):
                n = TILES[t][2]
                pe.wait_ge(s["h1p_ready"], max(t + 1, 2))
                mm(ps_x(t)[0:n, :], ident[0:n, 0:n], h1p[0:n, t, :], start=True, stop=False)

            def bus_spread(g):
                nb = G_IMAGES[g]
                pe.wait_ge(s["row_taken"], g + 1)
                for t in TILES_OF[g]:
                    _, t0, n = TILES[t]
                    at = t0 - G_AT[g]
                    mm(ps_x(t)[0:n, :], image_row[0:nb, at:at + n], row[0:nb, g, :],
                       start=(g > 0), stop=True).then_inc(s["x_ready"], 1)

            def transpose_y(t):
                n = TILES[t][2]
                pe.wait_ge(s["yhat_ready"], t + 1)
                transposes(lambda f: ps_yt(t)[:, f, :], yhat[:, t, :], n).then_inc(s["yt_ready"], 1)

            def mlp_up(i):
                g, m = divmod(i, MF)
                if m == 0:
                    pe.wait_ge(s["fhi_ready"], TILES_OF[g][-1] + 1)
                    pe.wait_ge(s["flo_ready"], TILES_OF[g][-1] + 1)
                if i >= len(FC_BANKS):
                    pe.wait_ge(s["relu_ready"], i - len(FC_BANKS) + 1)
                for k in range(DF):
                    at = slice(k * F + m * P, k * F + (m + 1) * P)
                    last = mm_split(ps_f(i), (wf_hi[:, at], wf_lo[:, at]),
                                    (f_hi[:, k, group_span(g)], f_lo[:, k, group_span(g)]),
                                    start=(k == 0), stop=(k == DF - 1))
                last.then_inc(s["fc_ready"], 1)

            def mlp_down(i, ms=range(MF)):
                t, c0, cols, _ = Y_PARTS[i]
                g, t0, n = TILES[t]
                if ms[0] == 0 and i == 1:
                    pe.wait_ge(s["row_taken"], 2)
                elif ms[0] == 0 and i == 2:
                    pe.wait_ge(s["h1_ready"], 4)
                elif ms[0] == 0 and i >= 4:
                    pe.wait_ge(s["result_ready"], i - 3)
                for m in ms:
                    if t == TILES_OF[g][0]:
                        j = MF * g + m
                        if j % 3 == 2:
                            pe.wait_ge(s["hidlo_dve"], (j + 1) // 3)
                        else:
                            pe.wait_ge(s["hidlo_pool"], by_pool(j + 1))
                    if m * D % WC == 0 and t == 0:
                        pe.wait_ge(s["wplo_ready"], m * D // WC + 1)
                    at = slice(m * D + c0, m * D + c0 + cols)
                    last = mm_split(ps_y(i), (hid_hi[:, m, t0:t0 + n], hid_lo[:, m, t0:t0 + n]),
                                    (wp_hi[:, at], wp_lo[:, at]), start=(m == 0), stop=(m == MF - 1))
                if ms[-1] == MF - 1:
                    last.then_inc(s["y_ready"], 1)

            pe.wait_ge(s["warm_ready"], 1)
            keep_warm(7, WARM)
            tokenizer_up(0, range(KP))
            tokenizer_up(1, range(2))
            pe.wait_ge(s["a_in"], 16)
            for t in TILES_OF[0]:
                tokenizer_down(t)
            tokenizer_up(1, range(2, KP - 1))
            pe.wait_ge(s["b_in"], 16)
            pe.wait_ge(s["c_in"], 16)
            for k in range(DF):
                last = mm(ps_lw, lmwo[:, k, :], mix[:, k, :], start=(k == 0), stop=(k == DF - 1))
            last.then_inc(s["lw_ready"], 1)
            pe.wait_ge(s["const_ready"], 9)
            transpose_x(0)
            transpose_x(1)
            tokenizer_up(1, [KP - 1])
            pe.wait_ge(s["h0_ready"], G_TILES[0])
            transpose_x(2)
            pe.wait_ge(s["xt_act"], 1)
            mm(ps_pe, publish_t, expand, start=True, stop=True).then_inc(s["pe_ready"], 1)
            queries_keys(0)
            tokenizer_down(3)
            router_up(0)
            pe.wait_ge(s["pad_ready"], 2 + NG)
            pe.wait_ge(s["pe_taken"], 1)
            pe.wait_ge(s["lw_taken"], 1)
            scores(0)
            tokenizer_down(4)
            values(0)
            router_logits(0)
            transpose_x(3)
            pe.wait_ge(s["h0_ready"], NT)
            mixer(0, 0, [0])
            arc_logits(0)
            mixer(0, 0, [1])
            transpose_x(4)
            mixer(0, 0, [2])
            pe.wait_ge(s["xt_act"], NT)
            transpose_probs(0)
            mixer(0, 1, [0])
            context(0)
            arc_transpose(0)
            mixer(0, 1, [1])
            router_up(1)
            mixer(0, 1, [2])
            mixer_end(0)
            router_logits(1)
            queries_keys(1)
            pe.wait_ge(s["pt_taken"], len(PT[0]))
            for f in range(DF):
                last = mm(ps_bus[:, f, :], compress_t[:, f * P:(f + 1) * P], pub_exp[:, :],
                          start=True, stop=True)
            last.then_inc(s["bus_ready"], 1)
            arc_logits(1)
            scores(1)
            keep_warm(0, 4)
            pe.wait_ge(s["lg_added"], NG)
            image_means(0)
            residual(0)
            bus_rows(0)
            arc_transpose(1)
            pe.wait_ge(s["q_taken"], 2)
            pe.wait_ge(s["k_taken"], 2)
            residual(1)
            residual(2)
            pe.wait_ge(s["sh_ready"], 2)
            bus_spread(0)
            values(1)
            mixer(1, 0)
            pe.wait_ge(s["arc_taken"], NG)
            for t in TILES_OF[0]:
                transpose_y(t)
            transpose_probs(1)
            mixer(1, 1)
            pe.wait_ge(s["wflo_ready"], DF * F // WC)
            for i in range(MF):
                mlp_up(i)
                if i == 0:
                    context(1)
                if i == 1:
                    mixer_end(1)
                if i == 6:
                    image_means(1)
            bus_rows(1)
            mlp_down(0)
            bus_spread(1)
            mlp_down(1)
            mlp_down(2, range(2))
            transpose_y(3)
            mlp_down(2, range(2, 3))
            transpose_y(4)
            mlp_down(2, range(3, MF))
            for i in range(MF, 2 * MF):
                mlp_up(i)
            mlp_down(3)
            mlp_down(4)

        @block.vector
        def _(dve):
            v = nc.vector
            for k in range(KP):
                dve.wait_ge(s["pwhi_ready"], k + 1)
                at = slice(k * W0 + D, (k + 1) * W0)
                v.tensor_tensor(pw_lo[:, at], pw[:, at], pw_hi[:, at].bitcast(F32),
                                ALU.subtract).then_inc(s["pwlo_ready"], 1)
            n1 = K1 * G_TOKENS[1]
            for h in range(2):
                dve.wait_ge(s["pwhi_ready"], KP + h + 1)
                at = slice(G1 + h * n1, G1 + (h + 1) * n1)
                v.tensor_tensor(pw_lo[:, at], pw[:, at], pw_hi[:, at].bitcast(F32),
                                ALU.subtract).then_inc(s["pwlo_ready"], 1)

            def h0_add(t):
                n = TILES[t][2]
                dve.wait_ge(s["h_ready"], t + 1)
                v.tensor_tensor(h0[0:n, t, :], ps_h(t)[0:n, :], b2[0:n, :], ALU.add).then_inc(s["h0_ready"], 1)

            def h0_stats(t):
                n = TILES[t][2]
                dve.wait_ge(s["h0_ready"], t + 1)
                v.bn_stats(stats[0:n, t, :], h0[0:n, t, :]).then_inc(s["stats_ready"], 1)

            def h0_moments(t):
                n = TILES[t][2]
                dve.wait_ge(s["stats_ready"], t + 1)
                v.bn_aggr(mv[0:n, t, :], stats[0:n, t, :]).then_inc(s["mv_ready"], 1)

            def h0_var(t):
                n = TILES[t][2]
                dve.wait_ge(s["mv_ready"], t + 1)
                v.scalar_tensor_tensor(ve[0:n, t, :], var_scale[0:n, :], mv[0:n, t, 1:2], var_shift[0:n, :],
                                       ALU.mult, ALU.add).then_inc(s["ve_ready"], 1)

            def neg_mean(t):
                n = TILES[t][2]
                dve.wait_ge(s["rs_ready"], t + 1)
                v.tensor_scalar(nm[0:n, t, :], rs[0:n, t, :], mv[0:n, t, 0:1], -1.0,
                                ALU.mult, ALU.mult).then_inc(s["nm_ready"], 1)

            def take_xt(t):
                _, t0, n = TILES[t]
                dve.wait_ge(s["xt_ready"], t + 1)
                v.tensor_scalar(xT[:, 1, t0:t0 + n], ps_xt(t, 1)[:, 0:n], w_in[:, 1:2], None,
                                ALU.mult).then_inc(s["xt_dve"], 1)

            def take_k(g):
                dve.wait_ge(s["qk_ready"], g + 1)
                v.tensor_copy(ks[:, group_span(g)], ps_qk[g][2 * DH:4 * DH, :]).then_inc(s["k_taken"], 1)

            def route_of(g):
                for f in range(DF):
                    last = v.tensor_reduce(route[:, f, images_of(g)],
                                           xT[:, f, group_span(g)].rearrange("p (b s) -> p b s", s=S),
                                           AX.X, ALU.add)
                last.then_inc(s["route_ready"], 1)

            def shift_scores(g):
                j0, n = PAIRS_OF[g][0], len(PAIRS_OF[g])
                for i in range(2):
                    dve.wait_ge(s["s_ready"], 2 * g + i + 1)
                    v.tensor_reduce(smax[:, i, j0:j0 + n], ps_s(g, i), AX.X, ALU.max).then_inc(s["smax_ready"], 1)
                for i in range(2):
                    dve.wait_ge(s["smax_ready"], 2 * g + i + 1)
                    last = v.tensor_tensor(sh[:, i, j0:j0 + n, :], ps_s(g, i),
                                           smax[:, i, j0:j0 + n].unsqueeze(2).to_broadcast([P, n, S]),
                                           ALU.subtract)
                last.then_inc(s["sh_ready"], 1)

            def scan(g, f):
                v.tensor_tensor_scan(ssm[:, f, group_span(g)], lam_scan[:, f, 0:G_TOKENS[g]],
                                     xT[:, f, group_span(g)], 0.0, ALU.mult, ALU.add).then_inc(s["ssm_ready"], 1)

            def probs_factors(g):
                j0, n = PAIRS_OF[g][0], len(PAIRS_OF[g])
                dve.wait_ge(s["se_ready"], g + 1)
                v.tensor_reduce(ssum[:, :, j0:j0 + n], se[:, :, j0:j0 + n, :], AX.X, ALU.add).then_inc(s["ssum_ready"], 1)
                dve.wait_ge(s["ssum_ready"], g + 1)
                v.reciprocal(srec[:, :, j0:j0 + n], ssum[:, :, j0:j0 + n]).then_inc(s["srec_ready"], 1)
                dve.wait_ge(s["srec_ready"], g + 1)
                v.tensor_scalar(sfac[:, j0:j0 + n], srec[:, 1, j0:j0 + n], neg_lam[:, :], None,
                                ALU.mult).then_inc(s["sfac_ready"], 1)

            def make_probs(g):
                j0, n = PAIRS_OF[g][0], len(PAIRS_OF[g])
                v.tensor_tensor(sp[:, 0, j0:j0 + n, :], se[:, 0, j0:j0 + n, :],
                                srec[:, 0, j0:j0 + n].unsqueeze(2).to_broadcast([P, n, S]),
                                ALU.mult).then_inc(s["sp_ready"], 1)
                dve.wait_ge(s["sfac_ready"], g + 1)
                v.tensor_tensor(sp[:, 1, j0:j0 + n, :], se[:, 1, j0:j0 + n, :],
                                sfac[:, j0:j0 + n].unsqueeze(2).to_broadcast([P, n, S]),
                                ALU.mult).then_inc(s["sp_ready"], 1)
                dve.wait_ge(s["sp_ready"], 2 * (g + 1))
                for r in range(2):
                    rows = slice(r * HALF, (r + 1) * HALF)
                    v.tensor_tensor(probs[rows, j0:j0 + n, r * S:(r + 1) * S], sp[rows, 0, j0:j0 + n, :],
                                    sp[rows, 1, j0:j0 + n, :], ALU.add).then_inc(s["probs_ready"], 1)

            def router_hidden(g):
                js = images_of(g)
                dve.wait_ge(s["rexp_ready"], g + 1)
                v.tensor_scalar(rden[:, js], rexp[:, js], 1.0, None, ALU.add).then_inc(s["rden_ready"], 1)
                dve.wait_ge(s["rden_ready"], g + 1)
                v.reciprocal(rrec[:, js], rden[:, js]).then_inc(s["rrec_ready"], 1)
                dve.wait_ge(s["rrec_ready"], g + 1)
                v.scalar_tensor_tensor(rhid[:, js], ps_hid(g), 1.0 / S, rrec[:, js],
                                       ALU.mult, ALU.mult).then_inc(s["rhid_ready"], 1)

            def router_shift(g):
                js, nb = images_of(g), G_IMAGES[g]
                dve.wait_ge(s["lg_ready"], g + 1)
                v.tensor_tensor(lg[:, js, :], ps_lg(g).rearrange("p j b -> p b j"),
                                rb2.unsqueeze(1).to_broadcast([P, nb, 3]), ALU.add).then_inc(s["lg_added"], 1)
                dve.wait_ge(s["lg_added"], g + 1)
                v.tensor_reduce(lgm[:, js], lg[:, js, :], AX.X, ALU.max).then_inc(s["lg_max"], 1)
                dve.wait_ge(s["lg_max"], g + 1)
                v.tensor_tensor(lgd[:, js, :], lg[:, js, :], lgm[:, js].unsqueeze(2).to_broadcast([P, nb, 3]),
                                ALU.subtract).then_inc(s["lg_shift"], 1)

            def router_gates(g):
                js = images_of(g)
                dve.wait_ge(s["lg_exp"], g + 1)
                v.tensor_reduce(lgs[:, js], lge[:, js, :], AX.X, ALU.add).then_inc(s["lg_sum"], 1)
                v.tensor_tensor(gsum[:, js], lge[:, js, 1], lge[:, js, 2], ALU.add).then_inc(s["lg_gsum"], 1)
                dve.wait_ge(s["lg_sum"], g + 1)
                v.reciprocal(lgr[:, js], lgs[:, js]).then_inc(s["lg_rec"], 1)
                dve.wait_ge(s["lg_rec"], g + 1)
                dve.wait_ge(s["lg_gsum"], g + 1)
                v.tensor_tensor(gate[:, js], gsum[:, js], lgr[:, js], ALU.mult).then_inc(s["gate_ready"], 1)
                v.tensor_tensor(p_full[:, js], lge[:, js, 2], lgr[:, js], ALU.mult).then_inc(s["pfull_ready"], 1)

            def arc_shift(g):
                nb = G_IMAGES[g]
                dve.wait_ge(s["arc_ready"], g + 1)
                v.tensor_reduce(arc_m[0:nb, g:g + 1], ps_arc(g), AX.X, ALU.max).then_inc(s["arcm_ready"], 1)
                dve.wait_ge(s["arcm_ready"], g + 1)
                v.tensor_scalar(arc_b[0:nb, g:g + 1], arc_m[0:nb, g:g + 1], -float(D) ** -0.5, None,
                                ALU.mult).then_inc(s["arcb_ready"], 1)

            def arc_probs(g):
                nb = G_IMAGES[g]
                dve.wait_ge(s["arce_ready"], g + 1)
                v.reciprocal(arc_r[0:nb, g:g + 1], arc_s[0:nb, g:g + 1]).then_inc(s["arcr_ready"], 1)
                dve.wait_ge(s["arcr_ready"], g + 1)
                v.tensor_scalar(arc_p[0:nb, g, :], arc_e[0:nb, g, :], arc_r[0:nb, g:g + 1], None,
                                ALU.mult).then_inc(s["arcp_ready"], 1)

            def gated_arc(g):
                dve.wait_ge(s["arct_ready"], g + 1)
                dve.wait_ge(s["pfull_ready"], g + 1)
                v.tensor_tensor(comb[0:SLOTS, G_AT[g] + S - 1:G_AT[g] + G_TOKENS[g]:S], ps_arct(g),
                                p_full[0:SLOTS, images_of(g)], ALU.mult).then_inc(s["arc_taken"], 1)

            def gated_context(g):
                b0, nb = G_FIRST[g], G_IMAGES[g]
                dve.wait_ge(s["gate_ready"], g + 1)
                dve.wait_ge(s["c_ready"], g + 1)
                v.tensor_tensor(comb[SLOTS:SLOTS + DH, group_span(g)].rearrange("p (b s) -> p b s", s=S),
                                ps_c(g).rearrange("p (b s) -> p b s", s=S),
                                gate[SLOTS:SLOTS + DH, b0:b0 + nb].unsqueeze(2).to_broadcast([DH, nb, S]),
                                ALU.mult).then_inc(s["c_taken"], 1)

            def rms_arg(t):
                n = TILES[t][2]
                dve.wait_ge(s["ssq_ready"], t + 1)
                v.tensor_scalar(rve[0:n, t:t + 1], ssq[0:n, t:t + 1], EPS_RMS, None,
                                ALU.add).then_inc(s["rve_ready"], 1)

            def mixer_out(t):
                n = TILES[t][2]
                dve.wait_ge(s["rr_ready"], t + 1)
                v.scalar_tensor_tensor(rms[0:n, t, :], ps_o(t)[0:n, :], rr[0:n, t:t + 1], w_out[0:n, :],
                                       ALU.mult, ALU.mult).then_inc(s["rms_ready"], 1)

            def mixer_add(t):
                n = TILES[t][2]
                dve.wait_ge(s["rms_ready"], t + 1)
                dve.wait_ge(s["a_ready"], t + 1)
                v.tensor_tensor(out2[0:n, t, :], rms[0:n, t, :], a[0:n, t, :], ALU.add).then_inc(s["out2_ready"], 1)

            def take_mean(g):
                nb = G_IMAGES[g]
                dve.wait_ge(s["m_ready"], g + 1)
                v.tensor_scalar(mean[:, g, :, 0:nb],
                                bank[5][:, 0:DF * NB].rearrange("p (f b) -> p f b", f=DF)[:, :, 0:nb],
                                1.0 / S, 0.1, ALU.mult, ALU.mult).then_inc(s["mean_ready"], 1)

            def h1_add(t):
                n = TILES[t][2]
                dve.wait_ge(s["x_ready"], t + 1)
                dve.wait_ge(s["h1p_ready"], t + 1)
                v.tensor_tensor(h1[0:n, t, :], ps_x(t)[0:n, :], h1p[0:n, t, :], ALU.add).then_inc(s["h1_ready"], 1)

            def h1_stats(t):
                n = TILES[t][2]
                dve.wait_ge(s["h1_ready"], t + 1)
                v.bn_stats(stats2[0:n, t, :], h1[0:n, t, :]).then_inc(s["stats2_ready"], 1)

            def h1_moments(t):
                n = TILES[t][2]
                dve.wait_ge(s["stats2_ready"], t + 1)
                v.bn_aggr(mv2[0:n, t, :], stats2[0:n, t, :]).then_inc(s["mv2_ready"], 1)

            def h1_var(t):
                n = TILES[t][2]
                dve.wait_ge(s["mv2_ready"], t + 1)
                v.tensor_scalar(ve2[0:n, t:t + 1], mv2[0:n, t, 1:2], EPS_LN, None, ALU.add).then_inc(s["ve2_ready"], 1)

            def make_yhat(t):
                n = TILES[t][2]
                dve.wait_ge(s["rs2_ready"], t + 1)
                v.tensor_scalar(yhat[0:n, t, :], h1[0:n, t, :], mv2[0:n, t, 0:1], rs2[0:n, t:t + 1],
                                ALU.subtract, ALU.mult).then_inc(s["yhat_ready"], 1)

            def f_low(t):
                _, t0, n = TILES[t]
                dve.wait_ge(s["fhi_ready"], t + 1)
                v.tensor_tensor(f_lo[:, :, t0:t0 + n], ps_yt(t)[:, :, 0:n], f_hi[:, :, t0:t0 + n].bitcast(F32),
                                ALU.subtract).then_inc(s["flo_ready"], 1)

            def square_of(i):
                g = i // MF
                dve.wait_ge(s["relu_ready"], i + 1)
                if i >= NBUF and (i - NBUF) % 3 != 2:
                    dve.wait_ge(s["hidlo_pool"], by_pool(i - NBUF + 1))
                elif i >= NBUF:
                    dve.wait_ge(s["hidlo_dve"], (i - NBUF + 1) // 3)
                v.tensor_tensor(square[:, i % NBUF, 0:G_TOKENS[g]], relu[:, i % NBUF, 0:G_TOKENS[g]],
                                relu[:, i % NBUF, 0:G_TOKENS[g]], ALU.mult).then_inc(s["square_ready"], 1)

            def hid_low(i):
                g, m = divmod(i, MF)
                dve.wait_ge(s["square_ready"], i + 1)
                dve.wait_ge(s["hidhi_ready"], i + 1)
                v.tensor_tensor(hid_lo[:, m, group_span(g)], square[:, i % NBUF, 0:G_TOKENS[g]],
                                hid_hi[:, m, group_span(g)].bitcast(F32),
                                ALU.subtract).then_inc(s["hidlo_dve"], 1)

            def spike_step(i, j):
                t, c0, cols, _ = Y_PARTS[i]
                n = TILES[t][2]
                count_, h1_, result_ = (x[0:n, t, c0:c0 + cols] for x in (count, h1, result))
                if j == 0:
                    dve.wait_ge(s["y_ready"], i + 1)
                    v.tensor_scalar(count_, ps_y(i), thresholds[0], None,
                                    ALU.is_gt).then_inc(s["count_ready"], 1)
                elif j < NUM_STEPS:
                    dve.wait_ge(s["count_ready"], NUM_STEPS * i + j)
                    v.scalar_tensor_tensor(count_, ps_y(i), thresholds[j], count_,
                                           ALU.is_gt, ALU.add).then_inc(s["count_ready"], 1)
                else:
                    dve.wait_ge(s["count_ready"], NUM_STEPS * (i + 1))
                    v.scalar_tensor_tensor(result_, count_, 1.0 / NUM_STEPS, h1_,
                                           ALU.mult, ALU.add).then_inc(s["result_ready"], 1)

            def spikes(i, first=0, end=NUM_STEPS + 1):
                for j in range(first, end):
                    spike_step(i, j)

            def last_spikes(i):
                t, c0, cols, _ = Y_PARTS[i]
                n, half = TILES[t][2], cols // 2
                done = NUM_STEPS * i
                for j in range(NUM_STEPS + 1):
                    for h in range(2):
                        at = slice(c0 + h * half, c0 + (h + 1) * half)
                        y_ = ps_y(i)[:, h * half:(h + 1) * half]
                        count_ = count[0:n, t, at]
                        if j == 0:
                            dve.wait_ge(s["y_ready"], i + 1)
                            v.tensor_scalar(count_, y_, thresholds[0], None,
                                            ALU.is_gt).then_inc(s["count_ready"], 1)
                        elif j < NUM_STEPS:
                            dve.wait_ge(s["count_ready"], done + 2 * (j - 1) + h + 1)
                            v.scalar_tensor_tensor(count_, y_, thresholds[j], count_,
                                                   ALU.is_gt, ALU.add).then_inc(s["count_ready"], 1)
                        else:
                            dve.wait_ge(s["count_ready"], done + 2 * (j - 1) + h + 1)
                            last = v.scalar_tensor_tensor(result[0:n, t, at], count_, 1.0 / NUM_STEPS,
                                                          h1[0:n, t, at], ALU.mult, ALU.add)
                last.then_inc(s["result_ready"], 1)

            dve.wait_ge(s["v_in"], 16)
            v.tensor_scalar(neg_lam[:, :], slr_lam, -1.0, None, ALU.mult).then_inc(s["neg_ready"], 1)
            dve.wait_ge(s["a_in"], 16)
            dve.wait_ge(s["const_ready"], 9)
            for i in range(5):
                if i < 3:
                    h0_add(i)
                if 1 <= i <= 3:
                    h0_moments(i - 1)
                if i < 3:
                    h0_stats(i)
                if 1 <= i <= 3:
                    h0_var(i - 1)
                if 2 <= i:
                    neg_mean(i - 2)
            for t in TILES_OF[0]:
                take_xt(t)
            dve.wait_ge(s["xt_act"], G_TILES[0])
            dve.wait_ge(s["xt_dve"], G_TILES[0])
            route_of(0)
            dve.wait_ge(s["lam_ready"], 2 * DF + 1)
            scan(0, 0)
            take_k(0)
            scan(0, 1)
            h0_add(3)
            h0_stats(3)
            router_hidden(0)
            h0_moments(3)
            h0_var(3)
            shift_scores(0)
            h0_add(4)
            neg_mean(3)
            h0_stats(4)
            dve.wait_ge(s["neg_ready"], 1)
            h0_moments(4)
            h0_var(4)
            probs_factors(0)
            neg_mean(4)
            dve.wait_ge(s["pad_ready"], 2 + NG)
            make_probs(0)
            router_shift(0)
            arc_shift(0)
            router_gates(0)
            dve.wait_ge(s["xt_act"], NT)
            route_of(1)
            arc_probs(0)
            gated_context(0)
            gated_arc(0)
            scan(1, 0)
            scan(1, 1)
            router_hidden(1)
            dve.wait_ge(s["b_in"], 16)
            rms_arg(0)
            rms_arg(1)
            mixer_out(0)
            rms_arg(2)
            mixer_out(1)
            mixer_add(0)
            take_k(1)
            mixer_out(2)
            mixer_add(1)
            router_shift(1)
            mixer_add(2)
            arc_shift(1)
            shift_scores(1)
            take_mean(0)
            router_gates(1)
            arc_probs(1)
            probs_factors(1)
            gated_arc(1)
            make_probs(1)
            h1_stats(0)
            h1_moments(0)
            h1_stats(1)
            h1_var(0)
            h1_moments(1)
            h1_stats(2)
            h1_var(1)
            h1_moments(2)
            h1_var(2)
            make_yhat(0)
            make_yhat(1)
            make_yhat(2)
            f_low(0)
            f_low(1)
            f_low(2)
            gated_context(1)
            square_of(0)
            square_of(1)
            rms_arg(3)
            rms_arg(4)
            square_of(2)
            hid_low(2)
            mixer_out(3)
            square_of(3)
            mixer_out(4)
            mixer_add(3)
            mixer_add(4)
            square_of(4)
            square_of(5)
            hid_low(5)
            take_mean(1)
            square_of(6)
            square_of(7)
            spikes(0, 0, 2)
            h1_add(3)
            h1_add(4)
            h1_stats(3)
            h1_moments(3)
            h1_stats(4)
            h1_var(3)
            h1_moments(4)
            spikes(0, 2, 3)
            h1_var(4)
            make_yhat(3)
            spikes(0, 3, 4)
            make_yhat(4)
            spikes(0, 4)
            f_low(3)
            f_low(4)
            spikes(1)
            later = [(2, j) for j in range(NUM_STEPS + 1)]
            for i in range(MF, NG * MF):
                square_of(i)
                if i > MF and i % 3 == 0:
                    hid_low(i - 1)
                elif later:
                    spike_step(*later.pop(0))
            for t, j in later:
                spike_step(t, j)
            spikes(3)
            last_spikes(4)


def lay_out(i):
    def chunks(w):
        w = np.asarray(w)
        return w.reshape(w.shape[0] // P, P, w.shape[1]).transpose(1, 0, 2)

    def flat(w):
        return chunks(w).reshape(P, -1)

    def rows(x, n):
        return np.broadcast_to(np.asarray(x).reshape(1, n), (P, n))

    x = np.asarray(i["x"]).reshape(B, 3, GRID, PATCH, GRID, PATCH)
    x = x.transpose(1, 3, 5, 0, 2, 4).reshape(KP * P, T)
    cols = [np.asarray(i[n]).reshape(DF, P).T for n in ("L0_tok_b1", "L0_attn_w_norm_in")]
    lam = np.repeat(np.asarray(i["L0_attn_lambdas"]), D // HEADS).reshape(DF, P).T
    qk = np.concatenate([np.asarray(i["L0_attn_slr_" + n]) for n in ("wq1", "wq2", "wk1", "wk2")], axis=1)
    lmwo = np.concatenate([np.asarray(i["L0_attn_landmarks"]), np.asarray(i["L0_attn_slr_wo"])], axis=0).T
    arrays = {
        "vectors": np.concatenate([*cols, lam, rows(i["L0_attn_router_b2"], 3),
                                   rows(i["L0_attn_slr_lam"], 1)], axis=1),
        "patches0_w1": np.concatenate([chunks(i["L0_tok_W1"]), chunks(x)[:, :, 0:G_TOKENS[0]]], axis=2).reshape(P, -1),
        "patches1": chunks(x)[:, :, G_TOKENS[0]:].reshape(P, -1),
        "pack_a": np.concatenate([flat(i["L0_tok_W2"]), rows(i["L0_tok_b2"], D)], axis=1),
        "pack_b": np.concatenate([flat(qk), flat(i["L0_attn_slr_wv"]), flat(i["L0_attn_router_w1"]), flat(lmwo),
                                  np.asarray(i["L0_attn_router_w2"]), rows(i["L0_attn_w_norm_out"], D)], axis=1),
        "pack_c": np.concatenate([flat(i["L0_attn_mix_w"]), np.asarray(i["L0_attn_bus_compress"]).T,
                                  np.asarray(i["L0_attn_bus_publish"]).T, np.asarray(i["L0_attn_bus_expand"])], axis=1),
        "w_fc": flat(np.asarray(i["L0_ffn_W_fc"]).T),
        "w_proj": flat(np.asarray(i["L0_ffn_W_proj"]).T),
    }
    return {n: np.ascontiguousarray(v) for n, v in arrays.items()}


def kernel(**inputs):
    import concourse.bacc as bacc
    from concourse.bass_utils import run_bass_kernel_spmd

    nc = bacc.Bacc("TRN2", target_bir_lowering=False, num_devices=1)
    arrays = {n + "_dram": v for n, v in lay_out(inputs).items()}
    args = [nc.dram_tensor(n, v.shape, mybir.dt.from_np(v.dtype), kind="ExternalInput").ap()
            for n, v in arrays.items()]
    out = nc.dram_tensor("out_dram", (T, D), F32, kind="ExternalOutput").ap()
    build(nc, *args, out)
    r = run_bass_kernel_spmd(nc, [arrays], core_ids=[0])
    return r.results[0]["out_dram"].reshape(B, S, D)
```
